# Optimizing a Trainium2 kernel written in Bass

```python
import numpy as np
import jax
import jax.numpy as jnp

def _softmax(x, axis=-1):
    return jax.nn.softmax(x, axis=axis)

def _gelu(x):
    return jax.nn.gelu(x, approximate=True)

def _silu(x):
    return jax.nn.silu(x)

def _sigmoid(x):
    return jax.nn.sigmoid(x)

def _layernorm(x, axis=-1, eps=1e-05):
    m = jnp.mean(x, axis=axis, keepdims=True)
    v = jnp.var(x, axis=axis, keepdims=True)
    return (x - m) / jnp.sqrt(v + eps)

def _scatter_add(tgt, idx, src, axis=0):
    return tgt.at[idx].add(src)

def _segment_sum(src, seg, n):
    return jax.ops.segment_sum(src, seg, n)
kernel_name = 'mk_metaformer_d1_conv_nchw768_r4_ed4381'

def setup_inputs(seed: int=0):
    np.random.seed(seed)
    _w = jnp.asarray

    def _rec_inputs():
        import jax
        import jax.numpy as jnp
        _gk = jax.random.key(seed)
        x = -0.0002221 + 1 * jax.random.normal(jax.random.fold_in(_gk, 1), (8, 192, 16, 16), jnp.float32)
        return x
    x = _rec_inputs()

    def _L0_conv_setup():
        import jax, jax.numpy as jnp
        import numpy as np
        WS = 8
        NH = 12
        DM = 192
        HD = DM // NH
        SCALE = float(HD) ** 0.5

        def _make_rel_coords():
            coords = np.stack(np.meshgrid(np.arange(WS), np.arange(WS), indexing='ij'))
            coords = coords.reshape(2, -1)
            rel = coords[:, :, None] - coords[:, None, :]
            rel = rel.transpose(1, 2, 0) + (WS - 1)
            rel[:, :, 0] *= 2 * WS - 1
            return jnp.asarray(rel.sum(-1), dtype=jnp.int32)
        key = jax.random.key(seed)
        ks = jax.random.split(key, 7)
        B, H, W = (8, 16, 16)
        return {'x': jax.random.normal(ks[0], (B, DM, H, W), dtype=jnp.float32), 'Wq': jax.random.normal(ks[1], (DM, DM), dtype=jnp.float32) * 0.02, 'Wk': jax.random.normal(ks[2], (DM, DM), dtype=jnp.float32) * 0.02, 'Wv': jax.random.normal(ks[3], (DM, DM), dtype=jnp.float32) * 0.02, 'Wo_w': jax.random.normal(ks[4], (DM, DM), dtype=jnp.float32) * 0.02, 'Wo_b': jax.random.normal(ks[5], (DM,), dtype=jnp.float32) * 0.02, 'rel_pos_bias': jax.random.normal(ks[6], (NH, (2 * WS - 1) ** 2), dtype=jnp.float32) * 0.02, 'rel_coords': _make_rel_coords()}
    _L0_conv_all = _L0_conv_setup()
    _L0_conv_in = {k: v for k, v in _L0_conv_all.items() if k in ('Wq', 'Wk', 'Wv', 'Wo_w', 'Wo_b', 'rel_pos_bias', 'rel_coords')}
    del _L0_conv_all

    def _L0_ffn_setup():
        import jax, jax.numpy as jnp
        import numpy as np
        B, S, H, F, E = (8, 128, 192, 768, 6)
        TOP_K = 2
        key = jax.random.key(seed)
        ks = jax.random.split(key, 7)
        sH = 1.0 / np.sqrt(H)
        sF = 1.0 / np.sqrt(F)
        return {'x': jax.random.normal(ks[0], (B, S, H), dtype=jnp.float32), 'gate_w': jax.random.normal(ks[1], (H, E), dtype=jnp.float32) * sH, 'gate_b': jax.random.normal(ks[2], (E,), dtype=jnp.float32) * 0.01, 'w1': jax.random.normal(ks[3], (E, H, F), dtype=jnp.float32) * sH, 'b1': jax.random.normal(ks[4], (E, F), dtype=jnp.float32) * 0.01, 'w2': jax.random.normal(ks[5], (E, F, H), dtype=jnp.float32) * sF, 'b2': jax.random.normal(ks[6], (E, H), dtype=jnp.float32) * 0.01}
    _L0_ffn_all = _L0_ffn_setup()
    _L0_ffn_in = {k: v for k, v in _L0_ffn_all.items() if k in ('gate_w', 'gate_b', 'w1', 'b1', 'w2', 'b2')}
    del _L0_ffn_all
    return {'x': x, 'L0_conv_Wq': _L0_conv_in['Wq'], 'L0_conv_Wk': _L0_conv_in['Wk'], 'L0_conv_Wv': _L0_conv_in['Wv'], 'L0_conv_Wo_w': _L0_conv_in['Wo_w'], 'L0_conv_Wo_b': _L0_conv_in['Wo_b'], 'L0_conv_rel_pos_bias': _L0_conv_in['rel_pos_bias'], 'L0_conv_rel_coords': _L0_conv_in['rel_coords'], 'L0_ffn_gate_w': _L0_ffn_in['gate_w'], 'L0_ffn_gate_b': _L0_ffn_in['gate_b'], 'L0_ffn_w1': _L0_ffn_in['w1'], 'L0_ffn_b1': _L0_ffn_in['b1'], 'L0_ffn_w2': _L0_ffn_in['w2'], 'L0_ffn_b2': _L0_ffn_in['b2']}

def reference(x, L0_conv_Wq, L0_conv_Wk, L0_conv_Wv, L0_conv_Wo_w, L0_conv_Wo_b, L0_conv_rel_pos_bias, L0_conv_rel_coords, L0_ffn_gate_w, L0_ffn_gate_b, L0_ffn_w1, L0_ffn_b1, L0_ffn_w2, L0_ffn_b2):
    import jax
    import jax.numpy as jnp

    def _L0_conv_ref(x, Wq, Wk, Wv, Wo_w, Wo_b, rel_pos_bias, rel_coords):
        import jax, jax.numpy as jnp
        import numpy as np
        WS = 8
        NH = 12
        DM = 192
        HD = DM // NH
        SCALE = float(HD) ** 0.5

        def _make_rel_coords():
            coords = np.stack(np.meshgrid(np.arange(WS), np.arange(WS), indexing='ij'))
            coords = coords.reshape(2, -1)
            rel = coords[:, :, None] - coords[:, None, :]
            rel = rel.transpose(1, 2, 0) + (WS - 1)
            rel[:, :, 0] *= 2 * WS - 1
            return jnp.asarray(rel.sum(-1), dtype=jnp.int32)
        B, C, H, W = x.shape
        nh, nw = (H // WS, W // WS)
        L = WS * WS
        xw = x.reshape(B, C, nh, WS, nw, WS).transpose(0, 2, 4, 3, 5, 1).reshape(B, nh, nw, L, C)

        def proj(Wm):
            y = jnp.einsum('bhwlc,oc->bhwlo', xw, Wm)
            return y.reshape(B, nh, nw, L, NH, HD).transpose(0, 1, 2, 4, 3, 5)
        q, k, v = (proj(Wq), proj(Wk), proj(Wv))
        bias = rel_pos_bias[:, rel_coords]
        attn = jnp.einsum('bhwnld,bhwnmd->bhwnlm', q, k) / SCALE + bias
        p = jax.nn.softmax(attn, axis=-1)
        o = jnp.einsum('bhwnlm,bhwnmd->bhwnld', p, v)
        o = o.reshape(B, nh, nw, NH, WS, WS, HD)
        o = o.transpose(0, 3, 6, 1, 4, 2, 5).reshape(B, C, H, W)
        return jnp.einsum('bchw,oc->bohw', o, Wo_w) + Wo_b[None, :, None, None]

    def _L0_ffn_ref(x, gate_w, gate_b, w1, b1, w2, b2):
        import jax, jax.numpy as jnp
        import numpy as np
        B, S, H, F, E = (8, 128, 192, 768, 6)
        TOP_K = 2
        b, s, h = x.shape
        xf = x.reshape(-1, h)
        gate_scores = xf @ gate_w + gate_b
        topk_scores, topk_idx = jax.lax.top_k(gate_scores, TOP_K)
        topk_weights = jax.nn.softmax(topk_scores, axis=1)
        hmid = jax.nn.gelu(jnp.einsum('nh,ehf->nef', xf, w1) + b1, approximate=False)
        expert_out = jnp.einsum('nef,efh->neh', hmid, w2) + b2
        sel = jnp.take_along_axis(expert_out, topk_idx[:, :, None], axis=1)
        out = jnp.einsum('nk,nkh->nh', topk_weights, sel)
        return out.reshape(b, s, h)

    def _gn(v, G=32, eps=1e-05):
        B_, C_, H_, W_ = v.shape
        g = v.reshape(B_, G, C_ // G, H_, W_)
        m = jnp.mean(g, axis=(2, 3, 4), keepdims=True)
        s = jnp.var(g, axis=(2, 3, 4), keepdims=True)
        return ((g - m) / jnp.sqrt(s + eps)).reshape(v.shape)

    def _ln_c(v, eps=1e-06):
        m = jnp.mean(v, axis=1, keepdims=True)
        s = jnp.var(v, axis=1, keepdims=True)
        return (v - m) / jnp.sqrt(s + eps)

    def _ln_t(v, eps=1e-05):
        m = jnp.mean(v, axis=-1, keepdims=True)
        s = jnp.var(v, axis=-1, keepdims=True)
        return (v - m) / jnp.sqrt(s + eps)

    def _to_tokens(v):
        B_, C_, H_, W_ = v.shape
        return v.reshape(B_, C_, H_ * W_).transpose(0, 2, 1)

    def _from_tokens(t, like):
        B_, C_, H_, W_ = like.shape
        return t.transpose(0, 2, 1).reshape(B_, C_, H_, W_)
    x = x + _L0_conv_ref(_ln_c(x), L0_conv_Wq, L0_conv_Wk, L0_conv_Wv, L0_conv_Wo_w, L0_conv_Wo_b, L0_conv_rel_pos_bias, L0_conv_rel_coords)
    t = _to_tokens(x)
    t = t + _L0_ffn_ref(_ln_t(t), L0_ffn_gate_w, L0_ffn_gate_b, L0_ffn_w1, L0_ffn_b1, L0_ffn_w2, L0_ffn_b2)
    x = _from_tokens(t, x)
    return x

_drawn_inputs = setup_inputs


def setup_inputs(seed=0):
    import zlib

    import numpy as np

    out = dict(_drawn_inputs(seed))
    spreads = {}
    factors = {'L0_conv_Wq': 8.0,
     'L0_conv_Wk': 8.0,
     'L0_conv_rel_pos_bias': 29.439,
     'L0_ffn_b1': 8.0,
     'L0_ffn_b2': 8.0}
    for name, (base, spread) in spreads.items():
        noise = np.random.default_rng([zlib.crc32(name.encode()), seed]).standard_normal(out[name].shape)
        drawn = base * np.exp(spread * noise) if base else spread * noise
        out[name] = jnp.asarray(drawn.astype(out[name].dtype))
    for name, factor in factors.items():
        out[name] = (out[name] * factor).astype(out[name].dtype)
    return out
```

```python
import concourse.bass as bass
from concourse import mybir
from contextlib import ExitStack
import numpy as np

B, C, IMG = 8, 192, 16
WIN = 8
L = WIN * WIN
NH, HD = 12, 16
P = 128
N = B * IMG * IMG
NT = N // P
CH = C // 2
PAIRS = CH // (2 * HD)
E, F = 6, 768
FT = F // P
NREL = (2 * WIN - 1) ** 2
CAP = N + P
PADROW = E * CAP
NBLK = (2 * N + E * (P - 1)) // P
ROW = C + 2
SKIP = 1 << 20
NCH = 2 * E
HW_F = F // 2
RC = 512

_at = {}
_n = 0
for _name, _w in (("ident", P), ("before", P), ("parity", 2), ("experts", 2 * E), ("region", E),
                  ("relrow", 2), ("low", 2), ("block", NBLK * E), ("upto", E * E), ("blockrow", NBLK)):
    _at[_name] = (_n, _n + _w)
    _n += _w
NCONST = _n


def constants():
    c = np.zeros((P, NCONST), np.float32)
    p = np.arange(P)

    def put(name, v):
        a, b = _at[name]
        c[:, a:b] = v

    put("ident", np.eye(P))
    put("before", p[:, None] < p[None, :])
    put("parity", (p[:, None] // HD) % 2 == np.arange(2)[None, :])
    put("experts", np.tile(np.arange(E), 2)[None, :])
    put("region", (np.arange(E) * CAP)[None, :])
    put("relrow", p[:, None] + P * np.arange(2)[None, :])
    low = np.zeros((P, 2))
    low[97, 0] = -1.0
    low[1, 1] = -1.0
    put("low", low)
    put("block", np.repeat(np.arange(NBLK), E)[None, :])
    put("upto", (np.arange(E)[None, :] <= np.arange(E)[:, None]).reshape(1, E * E))
    put("blockrow", (np.arange(NBLK) * P)[None, :])
    place = p[:, None, None] + P * np.arange(NT)[None, :, None] + N * np.arange(2)[None, None, :]
    places = np.concatenate([place.reshape(P, 2 * NT), np.full((P, 1), SKIP)], 1).astype(np.int32)
    return c, places


def program(nc, x, wqT, wkT, wvT, woT, wo_b, relT, coords, gate_w, gate_b, w1, b1, w2, b2,
            const_d, place_d, out):
    f32, f32r, i32, u32 = mybir.dt.float32, mybir.dt.float32r, mybir.dt.int32, mybir.dt.uint32
    ALU, ACT, AX = mybir.AluOpType, mybir.ActivationFunctionType, mybir.AxisListType
    NEG = -3.0e38

    bias_d = nc.dram_tensor("bias_d", [NH, L * L], f32, kind="Internal").ap()
    routed = nc.dram_tensor("routed", [PADROW + P, ROW], f32, kind="Internal").ap()
    made = nc.dram_tensor("made", [2 * N, C], f32, kind="Internal").ap()

    with ExitStack() as ctx:
        def sb(name, shape, dt=f32):
            return ctx.enter_context(nc.sbuf_tensor(name, shape, dt))

        def sem(name):
            return ctx.enter_context(nc.semaphore(name))

        cst = sb("cst", [P, NCONST])
        places = sb("places", [P, 2 * NT + 1], i32)
        wq, wk, wv = (sb(n, [CH, 2, C]) for n in ("wq", "wk", "wv"))
        wo = sb("wo", [CH + 1, 2, C])
        gw = sb("gw", [CH + 1, 2, E])
        w1h = sb("w1h", [CH + 2, NCH, F], f32r)
        w1l = sb("w1l", [CH + 2, NCH, F], f32r)
        w2s = sb("w2s", [P, E * FT, 2 * C], f32r)
        b2r = sb("b2r", [2, E * C], f32r)
        raw1 = sb("raw1", [CH + 2, F])
        raw2 = sb("raw2", [P, FT // 2, C])
        bias = sb("bias", [P, NH, L])
        ones = sb("ones", [P, P])
        ones2 = sb("ones2", [2, P], f32r)
        arena = sb("arena", [P, 3200])
        crd = [arena[:, n * RC:(n + 1) * RC].bitcast(i32) for n in range(2)]
        bT = [arena[0:NH, (2 + n) * RC:(3 + n) * RC] for n in range(2)]
        b2raw = arena[0:2, 4 * RC:4 * RC + E * C]
        back = arena[:, 0:8 * 2 * C].rearrange("p (n t k c) -> p n t k c", n=2, t=4, k=2)
        split = sb("split", [P, 4 * RC], f32r)
        hot = [split[:, n * 2 * RC:(n + 1) * 2 * RC].rearrange("p (k c) -> p k c", k=2) for n in range(2)]
        hTh = split[:, 0:F].rearrange("p (f t) -> p f t", f=FT)
        hTl = split[:, F:2 * F].rearrange("p (f t) -> p f t", f=FT)
        relraw = sb("relraw", [P, 2, NH])
        relh = sb("relh", [P, 2, NH], f32r)
        rell = sb("rell", [P, 2, NH], f32r)
        ytok = sb("ytok", [P, NT, C])
        xin = sb("xin", [CH, 2, P])
        xpad = sb("xpad", [P, ROW])
        xn = xpad[:, 0:C]
        xnT = sb("xnT", [CH, 2, P])
        qT = sb("qT", [CH, 2, P])
        kbd = sb("kbd", [CH, 2, 2, 2, L])
        vbd = [sb(f"vbd{n}", [P, 2, NH // 2, 2 * HD]) for n in range(2)]
        prob = [sb(f"prob{n}", [P, NH, L]) for n in range(2)]
        pT = sb("pT", [P, NH // 2, P])
        hid = pT[:, :, :].rearrange("p a b -> p (a b)")
        oT = sb("oT", [CH + 1, 2, P])
        rmax, rsum, rinv = (sb(n, [P, NH]) for n in ("rmax", "rsum", "rinv"))
        st, st2 = sb("st", [P, 6]), sb("st2", [P, 6])
        mv, mv2 = sb("mv", [P, 2]), sb("mv2", [P, 2])
        veps, veps2, rstd, rstd2, half_neg = (sb(n, [P, 1]) for n in ("veps", "veps2", "rstd", "rstd2", "half_neg"))
        row = [[sb(f"row{n}{k}", [P, ROW]) for k in range(2)] for n in range(2)]
        rowin = [row[n][0] for n in range(2)]
        yrow = [row[n][1] for n in range(2)]
        xlT = sb("xlT", [CH + 1, 2, P])
        score = sb("score", [P, 8])
        top = sb("top", [P, 8])
        topi = sb("topi", [P, 8], u32)
        topf = sb("topf", [P, 2])
        pick = [sb(f"pick{n}", [P, 2, E]) for n in range(2)]
        cnt = [sb(f"cnt{n}", [P, E]) for n in range(2)]
        seen = sb("seen", [P, E])
        slot_e = sb("slot_e", [P, E])
        slot_p = sb("slot_p", [P, 2, E])
        slot_f = sb("slot_f", [P, 2])
        slot = [sb(f"slot{n}", [P, 2], i32) for n in range(2)]
        tops = sb("tops", [P, NT, 2])
        gates = sb("gates", [P, 2, NT])
        gtmp = sb("gtmp", [P, NT])
        tot_i, nb_i, pad_i = (sb(n, [1, E], i32) for n in ("tot_i", "nb_i", "pad_i"))
        tot_f, nb_f, last_f, pad_f = (sb(n, [1, E]) for n in ("tot_f", "nb_f", "last_f", "pad_f"))
        tri = arena[0:1, 0:E * E].rearrange("p (a b) -> p a b", a=E)
        past, past_n = (arena[0:1, n * RC:n * RC + NBLK * E].rearrange("p (a b) -> p a b", a=NBLK) for n in (1, 2))
        exp_f, base_f, off_f = (sb(n, [1, NBLK]) for n in ("exp_f", "base_f", "off_f"))
        exp_i, off_i = (sb(n, [1, NBLK], i32) for n in ("exp_i", "off_i"))
        xTh, xTl = (split[0:CH + 2, 2 * F + n * 2 * P:2 * F + (n + 1) * 2 * P].rearrange("p (k t) -> p k t", k=2)
                    for n in range(2))
        ylow = prob[0][:, 6:9, :].rearrange("p a b -> p (a b)")
        ring = sb("ring", [P, NBLK], i32)
        dest = [sb(f"dest{n}", [P, 1], i32) for n in range(2)]
        z = [prob[n][:, 0:3, :].rearrange("p a b -> p (a b)") for n in range(2)]
        oc = [xnT, qT]

        bank = [ctx.enter_context(nc.psum_tensor(f"bank{n}", [P, 512], f32)) for n in range(4)]
        up_ps = ctx.enter_context(nc.psum_tensor("up_ps", [P, 4, 512], f32))
        s_ps = up_ps[:, 0:3, 0:2 * P]
        pTa = up_ps[:, 3, 0:3 * P]
        pTb = bank[3][:, 0:3 * P]

        ident = cst[:, slice(*_at["ident"])]
        before = cst[:, slice(*_at["before"])]
        parity = cst[:, slice(*_at["parity"])]
        experts = cst[:, slice(*_at["experts"])].rearrange("p (k e) -> p k e", k=2)
        region = cst[:, slice(*_at["region"])]
        relrow = cst[:, slice(*_at["relrow"])]
        low = cst[:, slice(*_at["low"])]

        s_const, s_bload = sem("s_const"), sem("s_bload")
        s_crd = [sem("s_crd0"), sem("s_crd1")]
        s_xin = sem("s_xin")
        s_raw = sem("s_raw")
        s_set, s_rel, s_apart = sem("s_set"), sem("s_rel"), sem("s_apart")
        s_b2 = sem("s_b2")
        s_hot, s_bmm, s_bev, s_bias = (sem(n) for n in ("s_hot", "s_bmm", "s_bev", "s_bias"))
        s_bout = [sem("s_bout0"), sem("s_bout1")]
        s_hi, s_lo, s_b1 = sem("s_hi"), sem("s_lo"), sem("s_b1")
        (p_x, p_xn, p_qk, p_v, p_s, p_pT, p_o, p_y, p_xl, p_gate, p_pos) = (
            sem(n) for n in ("p_x", "p_xn", "p_qk", "p_v", "p_s", "p_pT", "p_o", "p_y", "p_xl", "p_gate", "p_pos"))
        a_qk, a_exp, a_pT, a_o, a_xn, a_xl, a_row = (
            sem(n) for n in ("a_qk", "a_exp", "a_pT", "a_o", "a_xn", "a_xl", "a_row"))
        v_s, v_max, v_x, v_st, v_mv, v_xn, v_sum, v_inv, v_v = (
            sem(n) for n in ("v_s", "v_max", "v_x", "v_st", "v_mv", "v_xn", "v_sum", "v_inv", "v_v"))
        v_sc, v_top, v_topi, v_topf, v_pick, v_cnt = (
            sem(n) for n in ("v_sc", "v_top", "v_topi", "v_topf", "v_pick", "v_cnt"))
        v_y, v_st2, v_mv2, v_xl, v_pos, v_sp, v_sf, v_slot, v_seen = (
            sem(n) for n in ("v_y", "v_st2", "v_mv2", "v_xl", "v_pos", "v_sp", "v_sf", "v_slot", "v_seen"))
        g_sub, g_norm, g_ve, g_rs, g_ve2, g_rs2, g_dst = (
            sem(n) for n in ("g_sub", "g_norm", "g_ve", "g_rs", "g_ve2", "g_rs2", "g_dst"))
        s_scat = [sem("s_scat0"), sem("s_scat1")]
        p_tot, v_tab, v_gate, a_gate, s_pad = (sem(n) for n in ("p_tot", "v_tab", "v_gate", "a_gate", "s_pad"))
        s_rowin = [sem("s_rowin0"), sem("s_rowin1")]
        p_bx, p_up, p_hT, p_dn = (sem(n) for n in ("p_bx", "p_up", "p_hT", "p_dn"))
        a_hi, a_gelu, a_ylow = (sem(n) for n in ("a_hi", "a_gelu", "a_ylow"))
        v_lo, v_bxh, v_bx, v_ring, v_yrow = (sem(n) for n in ("v_lo", "v_bxh", "v_bx", "v_ring", "v_yrow"))
        s_made = [sem("s_made0"), sem("s_made1")]
        s_back = [sem("s_back0"), sem("s_back1")]
        v_z1, v_z, p_z, a_z = (sem(n) for n in ("v_z1", "v_z", "p_z", "a_z"))
        s_out = [sem("s_out0"), sem("s_out1")]

        FIRST, LAST = -2, NT + 2
        LOOP_A, LOOP_B = 2, NT // 2 - 1

        class Tile:

            def __init__(self, i, d):
                self.n, self.par, self.fixed = 2 * i + d, d % 2, isinstance(i, int)
                self.pair = i + d // 2

            def there(self, ahead=0):
                return not self.fixed or 0 <= self.n + ahead < NT

            def after(self, k):
                return not self.fixed or self.n >= k

        def wait_apart(eng, semaphore, value):
            eng.wait_ge(semaphore, value)
            eng.sem_inc(s_apart, 1)

        def windows(ap):
            return ap.rearrange("p (i w j) -> p w i j", i=WIN, w=2)

        def windowed(ap):
            return ap.rearrange("p (w i j) -> p w i j", w=2, i=WIN)

        w1_v = w1.rearrange("e (k p) f -> (e k) p f", p=CH)
        w2_v = w2.rearrange("e (k f p) n -> (e k) p f n", k=2, p=P)
        x_v = x.rearrange("b (k p) h w -> b p k (h w)", p=CH)
        out_v = out.rearrange("b (k p) h w -> b p k (h w)", p=CH)
        made_v = made.rearrange("(k t p) c -> t p k c", k=2, p=P)

        nc_block = ctx.enter_context(nc.Block())
        block = nc_block

        @block.sync
        def _(sp):
            for n in range(2):
                sp.dma_start(crd[n], coords[n * RC:(n + 1) * RC].partition_broadcast(P)).then_inc(s_crd[n], 16)

            def load_x(t):
                if not t.there():
                    return
                if t.after(1):
                    sp.wait_ge(p_x, t.n)
                sp.dma_start(xin[:, :, :], x_v[bass.ds(t.pair, 1), :, :, t.par * P:(t.par + 1) * P]
                             .rearrange("b p k n -> (b p) k n")).then_inc(s_xin, 16)

            def load_chunk(i, r):
                c = 2 * i + r
                if isinstance(i, int) and not 0 <= c < NCH:
                    return
                if not isinstance(i, int) or c >= 1:
                    sp.wait_ge(s_lo, c)
                    if r == 0:
                        sp.wait_ge(s_b1, i)
                sp.dma_start(raw1[0:CH, :], w1_v[bass.ds(c, 1), :, :].rearrange("a p f -> (a p) f")).then_inc(s_raw, 16)
                for k in range(2):
                    sp.dma_start(raw1[CH + k:CH + k + 1, :], b1[bass.ds(i, 1), :]).then_inc(s_raw, 16)
                sp.dma_start(raw2[:, :, :], w2_v[bass.ds(c, 1), :, :, :].rearrange("a p f n -> (a p) f n")).then_inc(s_raw, 16)

            load_x(Tile(0, 0))
            for n in range(2, 8):
                sp.wait_ge(s_hot, n - 1)
                sp.dma_start(crd[n % 2], coords[n * RC:(n + 1) * RC].partition_broadcast(P)).then_inc(s_crd[n % 2], 16)
            for n in range(2):
                sp.wait_ge(s_bout[n], 16 * 4)
            for w in range(2):
                sp.dma_start(bias[w * L:(w + 1) * L, :, :], bias_d.rearrange("h (l m) -> l h m", l=L)).then_inc(s_bias, 16)

            def slot_(i, r):
                load_x(Tile(i, r + 3))
                load_chunk(i, r)

            for s in range(FIRST, 2 * LOOP_A):
                slot_(s // 2, s % 2)
            with sp.Fori(LOOP_A, NCH // 2) as i:
                slot_(i, 0)
                slot_(i, 1)
            for s in range(NCH, LAST):
                slot_(s // 2, s % 2)

            sp.wait_ge(v_tab, 13)
            sp.wait_ge(g_dst, 3)
            for e in range(E):
                at = sp.value_load(pad_i[0:1, e:e + 1], min_val=e * CAP, max_val=e * CAP + N)
                sp.dma_start(routed[bass.ds(at, P), :], xpad[:, :]).then_inc(s_pad, 16)
            sp.dma_start(routed[PADROW:PADROW + P, :], xpad[:, :]).then_inc(s_pad, 16)
            for n in range(2):
                sp.wait_ge(s_scat[n], 32 * (NT // 2))
            sp.wait_ge(s_pad, 16 * (E + 1))

            def load_rows(b, par):
                if not isinstance(b, int) or b >= 2:
                    sp.wait_ge(v_ring, b - 1)
                at = sp.value_load(off_i[0:1, bass.ds(b, 1)], min_val=0, max_val=PADROW)
                sp.dma_start(rowin[par][:, :], routed[bass.ds(at, P), :]).then_inc(s_rowin[par], 16)

            load_rows(0, 0)
            load_rows(1, 1)
            with sp.Fori(1, NBLK // 2) as i:
                load_rows(2 * i, 0)
                load_rows(2 * i + 1, 1)
            if NBLK % 2:
                load_rows(NBLK - 1, 0)

            for n in range(2):
                sp.wait_ge(s_made[n], 16 * ((NBLK + 1 - n) // 2))
            def load_back(g):
                for k in range(2):
                    sp.dma_start(back[:, g % 2, :, k, :],
                                 made[k * N + 4 * g * P:k * N + 4 * (g + 1) * P, :].rearrange("(t p) c -> p t c", p=P)
                                 ).then_inc(s_back[g % 2], 16)

            load_back(0)
            load_back(1)
            for t in range(NT):
                if t % 4 == 0 and 8 <= t + 4 < NT:
                    sp.wait_ge(v_z, t)
                    load_back(t // 4 + 1)
                sp.wait_ge(a_z, t + 1)
                sp.dma_start(out_v[t // 2, :, :, (t % 2) * P:(t % 2 + 1) * P], oc[t % 2][:, :, :]).then_inc(s_out[t % 2], 16)
            for y in range(2):
                sp.wait_ge(s_out[y], 16 * B)

        @block.gpsimd
        def _(pool):
            pool.wait_ge(s_const, 16 * 3)
            for n in range(8):
                pool.wait_ge(s_crd[n % 2], 16 * (n // 2 + 1))
                if n >= 2:
                    pool.wait_ge(s_bmm, n - 1)
                for k in range(2):
                    ins = pool.tensor_scalar(hot[n % 2][:, k, :], crd[n % 2], relrow[:, k:k + 1], None, ALU.is_equal)
                ins.then_inc(s_hot, 1)

            def rstd_of(t, ready, mv_, veps_, rstd_, g_v, g_r, eps):
                if not t.there():
                    return
                wait_apart(pool, ready, t.n + 1)
                pool.tensor_scalar(veps_[:, :], mv_[:, 1:2], eps, None, ALU.add).then_inc(g_v, 1)
                pool.wait_ge(g_v, t.n + 1)
                pool.tensor_tensor(rstd_[:, :], veps_[:, :], half_neg[:, :], ALU.pow).then_inc(g_r, 1)

            def slot_(i, r):
                t = Tile(i, r)
                if t.there():
                    pool.wait_ge(v_max, t.n + 1)
                    p3 = prob[t.par][:, :, :]
                    pool.tensor_tensor(p3, p3, rmax[:, :].unsqueeze(2).to_broadcast([P, NH, L]),
                                       ALU.subtract).then_inc(g_sub, 1)
                rstd_of(Tile(i, r + 2), v_mv, mv, veps, rstd, g_ve, g_rs, 1e-6)
                if t.there():
                    pool.wait_ge(v_inv, t.n + 1)
                    pool.tensor_tensor(p3, p3, rinv[:, :].unsqueeze(2).to_broadcast([P, NH, L]),
                                       ALU.mult).then_inc(g_norm, 1)
                rstd_of(Tile(i, r - 1), v_mv2, mv2, veps2, rstd2, g_ve2, g_rs2, 1e-5)
                t = Tile(i, r - 2)
                if t.there():
                    pool.wait_ge(a_row, t.n + 1)
                    wait_apart(pool, v_slot, t.n + 1)
                    for k in range(2):
                        pool.indirect_dma_start(
                            out=routed[:, :], out_offset=bass.IndirectOffsetOnAxis(ap=slot[t.par][:, k:k + 1], axis=0),
                            in_=row[t.par][k][:, :], in_offset=None).then_inc(s_scat[t.par], 16)
                c = 2 * i + r
                if not isinstance(i, int) or 0 <= c < NCH:
                    pool.wait_ge(s_hi, c + 1)
                    pool.tensor_tensor(w1l[:, bass.ds(c, 1), :].rearrange("p a f -> p (a f)"), raw1[:, :],
                                       w1h[:, bass.ds(c, 1), :].rearrange("p a f -> p (a f)").bitcast(f32), ALU.subtract)
                    pool.tensor_tensor(w2s[:, bass.ds(c * (FT // 2), FT // 2), C:2 * C], raw2[:, :, :],
                                       w2s[:, bass.ds(c * (FT // 2), FT // 2), 0:C].bitcast(f32),
                                       ALU.subtract).then_inc(s_lo, 1)

            for s in range(FIRST, 2 * LOOP_A):
                slot_(s // 2, s % 2)
            with pool.Fori(LOOP_A, NCH // 2) as i:
                slot_(i, 0)
                slot_(i, 1)
            for s in range(NCH, LAST):
                slot_(s // 2, s % 2)
            pool.wait_ge(p_xn, NT)
            pool.memset(xpad[:, :], 0.0).then_inc(g_dst, 1)
            pool.wait_ge(g_dst, 1)
            pool.tensor_copy(xpad[:, C:C + 1].bitcast(i32), places[:, 2 * NT:2 * NT + 1]).then_inc(g_dst, 2)

            bound = pool.to_reg(2 * N - 1)

            def store_rows(b, par):
                wait_apart(pool, v_yrow, b + 1)
                pool.indirect_dma_start(
                    out=made[:, :], out_offset=bass.IndirectOffsetOnAxis(ap=dest[par][:, :], axis=0),
                    in_=yrow[par][:, 0:C], in_offset=None, bounds_check=bound, oob_is_err=False).then_inc(s_made[par], 16)

            with pool.Fori(0, NBLK // 2) as i:
                store_rows(2 * i, 0)
                store_rows(2 * i + 1, 1)
            if NBLK % 2:
                store_rows(NBLK - 1, 0)

        @block.scalar
        def _(act):
            act.dma_start(cst[:, :], const_d).then_inc(s_const, 16)
            act.dma_start(places[:, :], place_d).then_inc(s_const, 16)
            act.dma_start(relraw[:, 0, :], relT[0:P, :]).then_inc(s_const, 16)
            act.dma_start(relraw[0:NREL - P, 1, :], relT[P:NREL, :]).then_inc(s_bload, 16)
            for w_sb, w_dr in ((wq, wqT), (wk, wkT), (wv, wvT), (wo, woT), (gw, gate_w)):
                act.dma_start(w_sb[0:CH, :, :], w_dr.rearrange("(k p) n -> p k n", p=CH)).then_inc(s_bload, 16)
            act.dma_start(wo[CH:CH + 1, 1, :], wo_b.unsqueeze(0)).then_inc(s_bload, 16)
            act.dma_start(gw[CH:CH + 1, 1, :], gate_b.unsqueeze(0)).then_inc(s_bload, 16)
            for k in range(2):
                act.dma_start(b2raw[k:k + 1, :], b2.rearrange("(a e) n -> a (e n)", a=1)).then_inc(s_bload, 16)
            NLOAD = 16 * 10

            def bias_out(n):
                act.wait_ge(s_bmm, n + 1)
                if n >= 2:
                    act.wait_ge(s_bout[n % 2], 16 * (n // 2))
                act.activation(bT[n % 2], bank[n % 2][0:NH, :], ACT.Copy).then_inc(s_bev, 1)
                act.wait_ge(s_bev, n + 1)
                act.dma_start(bias_d[:, n * RC:(n + 1) * RC], bT[n % 2]).then_inc(s_bout[n % 2], 16)

            for n in range(8):
                bias_out(n)

            def slot_(i, r):
                t = Tile(i, r - 1)
                if t.there():
                    act.wait_ge(p_pT, t.n + 1)
                    if t.after(1):
                        act.wait_ge(p_o, t.n)
                    act.activation(pT[:, 0:3, :], pTa.rearrange("p (a b) -> p a b", a=3), ACT.Copy)
                    act.activation(pT[:, 3:6, :], pTb.rearrange("p (a b) -> p a b", a=3), ACT.Copy).then_inc(a_pT, 1)
                t = Tile(i, r - 2)
                if t.there():
                    act.wait_ge(p_xl, t.n + 1)
                    if t.after(1):
                        act.wait_ge(p_gate, t.n)
                    act.activation(xlT[0:CH, :, :], bank[1][0:CH, 0:2 * P].rearrange("p (k n) -> p k n", k=2),
                                   ACT.Copy).then_inc(a_xl, 1)
                    if t.after(2):
                        act.wait_ge(s_scat[t.par], 32 * t.pair)
                    act.activation(row[t.par][1][:, 0:C], row[t.par][0][:, 0:C], ACT.Copy).then_inc(a_row, 1)
                t = Tile(i, r)
                if t.there():
                    act.wait_ge(g_sub, t.n + 1)
                    p3 = prob[t.par][:, :, :]
                    act.activation(p3, p3, ACT.Exp).then_inc(a_exp, 1)
                t = Tile(i, r + 1)
                if t.there():
                    act.wait_ge(p_qk, t.n + 1)
                    if t.after(1):
                        act.wait_ge(p_s, t.n)
                    act.activation(qT[:, :, :], bank[2][0:CH, 0:2 * P].rearrange("p (k n) -> p k n", k=2),
                                   ACT.Copy, scale=float(HD) ** -0.5)
                    for h in range(2):
                        ins = act.activation(kbd[:, :, :, h, :],
                                             bank[2][0:CH, 2 * P:4 * P].rearrange("p (k w m) -> p k w m", k=2, w=2),
                                             ACT.Copy, scale=parity[0:CH, h:h + 1])
                    ins.then_inc(a_qk, 1)
                t = Tile(i, r - 1)
                if t.there():
                    act.wait_ge(p_o, t.n + 1)
                    if t.after(1):
                        act.wait_ge(p_y, t.n)
                    for k in range(2):
                        ins = act.activation(windows(oT[0:CH, k, :]), windowed(bank[1][0:CH, k * P:(k + 1) * P]), ACT.Copy)
                    ins.then_inc(a_o, 1)
                t = Tile(i, r + 2)
                if t.there():
                    act.wait_ge(p_xn, t.n + 1)
                    if t.after(1):
                        act.wait_ge(p_v, t.n)
                    for k in range(2):
                        ins = act.activation(windowed(xnT[:, k, :]), windows(bank[0][0:CH, k * P:(k + 1) * P]), ACT.Copy)
                    ins.then_inc(a_xn, 1)
                c = 2 * i + r
                if not isinstance(i, int) or 0 <= c < NCH:
                    act.wait_ge(s_raw, 64 * (c + 1))
                    act.activation(w1h[:, bass.ds(c, 1), :].rearrange("p a f -> p (a f)"), raw1[:, :], ACT.Copy)
                    act.activation(w2s[:, bass.ds(c * (FT // 2), FT // 2), 0:C], raw2[:, :, :],
                                   ACT.Copy).then_inc(s_hi, 1)

            for s in range(FIRST, 2 * LOOP_A):
                slot_(s // 2, s % 2)
            with act.Fori(LOOP_A, NCH // 2) as i:
                slot_(i, 0)
                slot_(i, 1)
            for s in range(NCH, LAST):
                slot_(s // 2, s % 2)
            act.wait_ge(v_gate, 1)
            act.activation(gates[:, 1, :], gtmp[:, :], ACT.Exp).then_inc(a_gate, 1)

            def gelu(b):
                act.wait_ge(p_up, b + 1)
                if not isinstance(b, int) or b >= 1:
                    act.wait_ge(p_hT, b)
                act.activation(hid.rearrange("p (n c) -> p n c", n=2), up_ps[:, 0:2, 0:HW_F], ACT.Gelu).then_inc(a_gelu, 1)

            def hi(b):
                act.wait_ge(p_hT, b + 1)
                if not isinstance(b, int) or b >= 1:
                    act.wait_ge(p_dn, b)
                for n in range(2):
                    act.activation(hTh[:, 3 * n:3 * n + 3, :], up_ps[:, 2 + n, 0:3 * P].rearrange("p (a b) -> p a b", a=3),
                                   ACT.Copy).then_inc(a_hi, 1)

            def ylow_(b):
                act.wait_ge(p_dn, b + 1)
                if not isinstance(b, int) or b >= 1:
                    act.wait_ge(v_yrow, b)
                act.activation(ylow[:, :], bank[1][:, C:2 * C], ACT.Copy).then_inc(a_ylow, 1)

            gelu(0)
            hi(0)
            gelu(1)
            ylow_(0)
            with act.Fori(1, NBLK - 1) as b:
                hi(b)
                gelu(b + 1)
                ylow_(b)
            hi(NBLK - 1)
            ylow_(NBLK - 1)

            def last(t, par):
                act.wait_ge(p_z, t + 1)
                if not isinstance(t, int) or t >= 2:
                    act.wait_ge(s_out[par], 16 * (t // 2 if isinstance(t, int) else t_pair(t)))
                act.activation(oc[par][:, :, :], bank[2 + par][0:CH, 0:2 * P].rearrange("p (k n) -> p k n", k=2),
                               ACT.Copy).then_inc(a_z, 1)

            pair_of = {}

            def t_pair(t):
                return pair_of["i"]

            last(0, 0)
            last(1, 1)
            with act.Fori(1, NT // 2) as i:
                pair_of["i"] = i
                last(2 * i, 0)
                last(2 * i + 1, 1)

        @block.vector
        def _(dve):
            dve.memset(ones[:, :], 1.0)
            dve.memset(ones2[:, :].bitcast(f32), 1.0)
            dve.memset(oT[CH:CH + 1, :, :], 1.0)
            dve.memset(xlT[CH:CH + 1, :, :], 1.0)
            dve.memset(half_neg[:, :], -0.5)
            for n in range(2):
                dve.memset(vbd[n][:, :, :, :], 0.0)
                for k in range(2):
                    dve.memset(row[n][k][:, C:ROW], 0.0)
            dve.memset(score[:, :], NEG)
            dve.memset(seen[:, :], 0.0).then_inc(s_set, 1)
            dve.wait_ge(s_set, 1)
            dve.wait_ge(s_const, 16 * 3)
            dve.wait_ge(s_bload, 16 * 10)
            dve.tensor_copy(relh[:, 0, :], relraw[:, 0, :])
            dve.tensor_copy(relh[0:NREL - P, 1, :], relraw[0:NREL - P, 1, :])
            dve.tensor_copy(b2r[:, :], b2raw).then_inc(s_b2, 1)
            dve.wait_ge(s_b2, 1)
            dve.tensor_tensor(rell[:, 0, :], relraw[:, 0, :], relh[:, 0, :].bitcast(f32), ALU.subtract)
            dve.tensor_tensor(rell[0:NREL - P, 1, :], relraw[0:NREL - P, 1, :],
                              relh[0:NREL - P, 1, :].bitcast(f32), ALU.subtract).then_inc(s_rel, 1)
            dve.scalar_tensor_tensor(out=b2r[:, :], in0=b2r[:, :].bitcast(f32), scalar=low[0:2, 1:2], in1=b2raw,
                                     op0=ALU.mult, op1=ALU.add).then_inc(s_b2, 1)

            def slot_(i, r):
                t = Tile(i, r)
                if t.there():
                    if t.fixed and t.n == 0:
                        dve.wait_ge(s_bias, 32)
                    dve.wait_ge(p_s, t.n + 1)
                    if t.after(2):
                        dve.wait_ge(p_pT, t.n - 1)
                    pr = prob[t.par][:, :, :]
                    for k in range(2):
                        ins = dve.tensor_tensor(pr[:, 6 * k:6 * k + 6, :].rearrange("p (j h) m -> p j (h m)", j=PAIRS),
                                                s_ps[:, :, k * P:(k + 1) * P],
                                                bias[:, 6 * k:6 * k + 6, :].rearrange("p (j h) m -> p j (h m)", j=PAIRS),
                                                ALU.add)
                    ins.then_inc(v_s, 1)
                    dve.wait_ge(v_s, t.n + 1)
                    if t.after(1):
                        dve.wait_ge(g_sub, t.n)
                    dve.tensor_reduce(rmax[:, :], pr, AX.X, ALU.max).then_inc(v_max, 1)
                t = Tile(i, r + 2)
                if t.there():
                    dve.wait_ge(p_x, t.n + 1)
                    dve.tensor_copy(ytok[:, bass.ds(t.n, 1), :].rearrange("p a c -> p (a c)"), bank[0][:, 0:C])
                    if t.after(1):
                        wait_apart(dve, v_mv, t.n)
                    dve.bn_stats(st[:, :], bank[0][:, 0:C]).then_inc(v_x, 1)
                    if t.after(1):
                        dve.wait_ge(g_ve, t.n)
                        dve.wait_ge(v_xn, t.n)
                    wait_apart(dve, v_x, t.n + 1)
                    dve.bn_aggr(mv[:, :], st[:, :]).then_inc(v_mv, 1)
                    dve.wait_ge(g_rs, t.n + 1)
                    if t.after(1):
                        dve.wait_ge(p_xn, t.n)
                    dve.tensor_scalar(xn[:, :], ytok[:, bass.ds(t.n, 1), :].rearrange("p a c -> p (a c)"),
                                      mv[:, 0:1], rstd[:, 0:1], ALU.subtract, ALU.mult).then_inc(v_xn, 1)
                t = Tile(i, r)
                if t.there():
                    dve.wait_ge(a_exp, t.n + 1)
                    if t.after(1):
                        dve.wait_ge(v_inv, t.n)
                    dve.tensor_reduce(rsum[:, :], pr, AX.X, ALU.add).then_inc(v_sum, 1)
                    dve.wait_ge(v_sum, t.n + 1)
                    if t.after(1):
                        dve.wait_ge(g_norm, t.n)
                    dve.reciprocal(rinv[:, :], rsum[:, :]).then_inc(v_inv, 1)
                t = Tile(i, r + 1)
                if t.there():
                    dve.wait_ge(p_v, t.n + 1)
                    if t.after(2):
                        dve.wait_ge(p_o, t.n - 1)
                    for h in range(2):
                        for w in range(2):
                            ins = dve.tensor_copy(
                                vbd[t.par][h * L:(h + 1) * L, w, :, h * HD:(h + 1) * HD],
                                bank[3][w * L:(w + 1) * L, 0:C].rearrange("p (j h d) -> p j h d", h=2, d=HD)[:, :, h, :])
                    ins.then_inc(v_v, 1)
                t = Tile(i, r - 2)
                if t.there():
                    dve.wait_ge(p_gate, t.n + 1)
                    if t.after(1):
                        dve.wait_ge(v_topi, t.n)
                    dve.tensor_copy(score[:, 0:E], bank[0][:, 0:E]).then_inc(v_sc, 1)
                    wait_apart(dve, v_sc, t.n + 1)
                    dve.max(top[:, :], score[:, :]).then_inc(v_top, 1)
                    wait_apart(dve, v_top, t.n + 1)
                    dve.max_index(topi[:, :], top[:, :], score[:, :]).then_inc(v_topi, 1)
                    dve.tensor_copy(tops[:, bass.ds(t.n, 1), :].rearrange("p a k -> p (a k)"), top[:, 0:2])
                    dve.wait_ge(v_topi, t.n + 1)
                    dve.tensor_copy(topf[:, :], topi[:, 0:2]).then_inc(v_topf, 1)
                    dve.wait_ge(v_topf, t.n + 1)
                    dve.tensor_tensor(pick[t.par][:, :, :], experts, topf[:, :].unsqueeze(2).to_broadcast([P, 2, E]),
                                      ALU.is_equal).then_inc(v_pick, 1)
                    dve.wait_ge(v_pick, t.n + 1)
                    if t.after(1):
                        dve.wait_ge(p_pos, t.n)
                    dve.tensor_tensor(cnt[t.par][:, :], pick[t.par][:, 0, :], pick[t.par][:, 1, :],
                                      ALU.add).then_inc(v_cnt, 1)
                t = Tile(i, r - 1)
                if t.there():
                    dve.wait_ge(p_y, t.n + 1)
                    yt = ytok[:, bass.ds(t.n, 1), :].rearrange("p a c -> p (a c)")
                    dve.tensor_tensor(yt, bank[1][:, 0:C], yt, ALU.add).then_inc(v_y, 1)
                    if t.after(1):
                        dve.wait_ge(v_mv2, t.n)
                    wait_apart(dve, v_y, t.n + 1)
                    dve.bn_stats(st2[:, :], yt).then_inc(v_st2, 1)
                    if t.after(1):
                        dve.wait_ge(g_ve2, t.n)
                        dve.wait_ge(v_xl, t.n)
                    wait_apart(dve, v_st2, t.n + 1)
                    dve.bn_aggr(mv2[:, :], st2[:, :]).then_inc(v_mv2, 1)
                t = Tile(i, r - 2)
                if t.there():
                    dve.wait_ge(p_pos, t.n + 1)
                    if t.after(1):
                        dve.wait_ge(v_sp, t.n)
                    dve.tensor_tensor(slot_e[:, :], bank[0][:, 0:E], region, ALU.add).then_inc(v_pos, 1)
                    dve.wait_ge(v_pos, t.n + 1)
                    if t.after(1):
                        dve.wait_ge(v_sf, t.n)
                    dve.tensor_tensor(slot_p[:, :, :], pick[t.par][:, :, :],
                                      slot_e[:, :].unsqueeze(1).to_broadcast([P, 2, E]), ALU.mult).then_inc(v_sp, 1)
                    dve.tensor_tensor(seen[:, :], seen[:, :], cnt[t.par][:, :], ALU.add).then_inc(v_seen, 1)
                    dve.wait_ge(v_sp, t.n + 1)
                    dve.tensor_reduce(slot_f[:, :], slot_p[:, :, :], AX.X, ALU.add).then_inc(v_sf, 1)
                    dve.wait_ge(v_sf, t.n + 1)
                    if t.after(2):
                        dve.wait_ge(s_scat[t.par], 32 * t.pair)
                    for k in range(2):
                        dve.tensor_copy(row[t.par][k][:, C:C + 1].bitcast(i32), places[:, bass.ds(2 * t.n + k, 1)])
                    dve.tensor_copy(slot[t.par][:, :], slot_f[:, :]).then_inc(v_slot, 1)
                t = Tile(i, r - 1)
                if t.there():
                    dve.wait_ge(g_rs2, t.n + 1)
                    if t.after(2):
                        dve.wait_ge(s_scat[t.par], 32 * t.pair)
                    dve.tensor_scalar(row[t.par][0][:, 0:C], yt, mv2[:, 0:1], rstd2[:, 0:1],
                                      ALU.subtract, ALU.mult).then_inc(v_xl, 1)
                c = 2 * i + r
                if r == 1 and (not isinstance(i, int) or 0 <= c < NCH):
                    dve.wait_ge(s_lo, c + 1)
                    wb = w1h[CH:CH + 2, bass.ds(c, 1), :].rearrange("p a f -> p (a f)")
                    dve.scalar_tensor_tensor(out=wb, in0=wb.bitcast(f32), scalar=low[CH:CH + 2, 0:1], in1=raw1[CH:CH + 2, :],
                                             op0=ALU.mult, op1=ALU.add).then_inc(s_b1, 1)

            for s in range(FIRST, 2 * LOOP_A):
                slot_(s // 2, s % 2)
            with dve.Fori(LOOP_A, NCH // 2) as i:
                slot_(i, 0)
                slot_(i, 1)
            for s in range(NCH, LAST):
                slot_(s // 2, s % 2)

            step = [0]

            def then(ins):
                step[0] += 1
                ins.then_inc(v_tab, 1)
                dve.wait_ge(v_tab, step[0])

            def c1(name):
                return cst[0:1, slice(*_at[name])]

            dve.wait_ge(p_tot, 1)
            dve.tensor_tensor(pad_f[:, :], bank[0][0:1, 0:E], c1("region"), ALU.add)
            then(dve.tensor_scalar(tot_f[:, :], bank[0][0:1, 0:E], float(P - 1), None, ALU.add))
            dve.tensor_copy(pad_i[:, :], pad_f[:, :])
            then(dve.tensor_copy(tot_i[:, :], tot_f[:, :]))
            then(dve.tensor_scalar(nb_i[:, :], tot_i[:, :], 7, None, ALU.arith_shift_right))
            then(dve.tensor_copy(nb_f[:, :], nb_i[:, :]))
            nbb = nb_f[:, :].unsqueeze(1)
            then(dve.tensor_tensor(tri[:, :, :], c1("upto").rearrange("p (a b) -> p a b", a=E),
                                   nbb.to_broadcast([1, E, E]), ALU.mult))
            then(dve.tensor_reduce(last_f[:, :], tri[:, :, :], AX.X, ALU.add))
            then(dve.tensor_tensor(past[:, :, :], c1("block").rearrange("p (a b) -> p a b", a=NBLK),
                                   last_f[:, :].unsqueeze(1).to_broadcast([1, NBLK, E]), ALU.is_ge))
            then(dve.tensor_tensor(past_n[:, :, :], past[:, :, :], nbb.to_broadcast([1, NBLK, E]), ALU.mult))
            dve.tensor_reduce(exp_f[:, :], past[:, :, :], AX.X, ALU.add)
            then(dve.tensor_reduce(base_f[:, :], past_n[:, :, :], AX.X, ALU.add))
            then(dve.scalar_tensor_tensor(out=off_f[:, :], in0=base_f[:, :], scalar=-float(P), in1=c1("blockrow"),
                                          op0=ALU.mult, op1=ALU.add))
            then(dve.scalar_tensor_tensor(out=base_f[:, :], in0=exp_f[:, :], scalar=float(CAP), in1=off_f[:, :],
                                          op0=ALU.mult, op1=ALU.add))
            dve.tensor_scalar(off_i[:, :], base_f[:, :], float(PADROW), None, ALU.min)
            then(dve.tensor_scalar(exp_i[:, :], exp_f[:, :], float(E - 1), None, ALU.min))
            dve.tensor_tensor(gtmp[:, :], tops[:, :, 1], tops[:, :, 0], ALU.subtract).then_inc(v_gate, 1)
            dve.wait_ge(a_gate, 1)
            then(dve.tensor_scalar(gtmp[:, :], gates[:, 1, :], 1.0, None, ALU.add))
            dve.wait_ge(v_gate, 1)
            dve.reciprocal(gates[:, 0, :], gtmp[:, :]).then_inc(v_gate, 1)
            dve.wait_ge(v_gate, 2)
            dve.tensor_tensor(gates[:, 1, :], gates[:, 1, :], gates[:, 0, :], ALU.mult).then_inc(v_gate, 1)

            dve.memset(xTh[CH:CH + 2, :, :].bitcast(f32), 1.0)

            def x_parts(b, par):
                dve.wait_ge(p_bx, b + 1)
                if not isinstance(b, int) or b >= 1:
                    dve.wait_ge(p_up, b)
                xps = bank[0][0:CH, 0:2 * P].rearrange("p (k n) -> p k n", k=2)
                dve.tensor_copy(xTh[0:CH, :, :], xps).then_inc(v_bxh, 1)
                dve.tensor_copy(ring[:, bass.ds(b, 1)], rowin[par][:, C:C + 1].bitcast(i32)).then_inc(v_ring, 1)
                dve.wait_ge(v_bxh, b + 1)
                dve.tensor_tensor(xTl[0:CH, :, :], xps, xTh[0:CH, :, :].bitcast(f32), ALU.subtract).then_inc(v_bx, 1)

            def lo(b):
                for n in range(2):
                    dve.wait_ge(a_hi, 2 * b + n + 1)
                    dve.tensor_tensor(hTl[:, 3 * n:3 * n + 3, :], up_ps[:, 2 + n, 0:3 * P].rearrange("p (a b) -> p a b", a=3),
                                      hTh[:, 3 * n:3 * n + 3, :].bitcast(f32), ALU.subtract).then_inc(v_lo, 1)

            def y_out(b, par, turn):
                dve.wait_ge(a_ylow, b + 1)
                if not isinstance(b, int) or b >= 2:
                    dve.wait_ge(s_made[par], 16 * turn)
                dve.wait_ge(v_ring, b + 1)
                dve.tensor_copy(dest[par][:, :], ring[:, bass.ds(b, 1)])
                dve.tensor_tensor(yrow[par][:, 0:C], bank[1][:, 0:C], ylow[:, :], ALU.add).then_inc(v_yrow, 1)

            x_parts(0, 0)
            x_parts(1, 1)

            def blk(b, par, turn):
                lo(b)
                if not isinstance(b, int) or b + 2 < NBLK:
                    x_parts(b + 2, par)
                y_out(b, par, turn)

            blk(0, 0, 0)
            blk(1, 1, 0)
            with dve.Fori(1, (NBLK - 2) // 2) as i:
                blk(2 * i, 0, i)
                blk(2 * i + 1, 1, i)
            for b in range((NBLK - 2) // 2 * 2, NBLK):
                blk(b, b % 2, b // 2)

            def fin(t, par, g):
                n = t - 4 * g
                if n == 0:
                    dve.wait_ge(s_back[g % 2], 32 * (g // 2 + 1))
                if t >= 2:
                    dve.wait_ge(p_z, t - 1)
                dve.scalar_tensor_tensor(out=z[par], in0=back[:, g % 2, n, 0, :], scalar=gates[:, 0, t:t + 1],
                                         in1=ytok[:, t, :], op0=ALU.mult, op1=ALU.add).then_inc(v_z1, 1)
                dve.wait_ge(v_z1, t + 1)
                dve.scalar_tensor_tensor(out=z[par], in0=back[:, g % 2, n, 1, :], scalar=gates[:, 1, t:t + 1],
                                         in1=z[par], op0=ALU.mult, op1=ALU.add).then_inc(v_z, 1)

            dve.wait_ge(v_gate, 3)
            for t in range(NT):
                fin(t, t % 2, t // 4)

        @block.tensor
        def _(pe):
            def mm(o, a, b_, start=True, stop=True):
                return pe.matmul(o, a, b_, start=start, stop=stop)

            pe.wait_ge(s_rel, 1)
            for n in range(8):
                pe.wait_ge(s_hot, n + 1)
                if n >= 2:
                    pe.wait_ge(s_bev, n - 1)
                for k, rows in ((0, P), (1, NREL - P)):
                    for part in (relh, rell):
                        ins = mm(bank[n % 2][0:NH, :], part[0:rows, k, :], hot[n % 2][0:rows, k, :],
                                 start=(k == 0 and part is relh), stop=(k == 1 and part is rell))
                ins.then_inc(s_bmm, 1)
            pe.wait_ge(s_bev, 8)
            pe.wait_ge(s_set, 1)
            pe.wait_ge(s_bload, 16 * 10)

            def slot_(i, r):
                t = Tile(i, r)
                if t.there():
                    pe.wait_ge(a_qk, t.n + 1)
                    if t.after(1):
                        pe.wait_ge(v_s, t.n)
                    for half in range(2):
                        for j in range(PAIRS):
                            for w in range(2):
                                ins = mm(s_ps[w * L:(w + 1) * L, j, half * P:(half + 1) * P],
                                         qT[32 * j:32 * j + 32, half, w * L:(w + 1) * L],
                                         kbd[32 * j:32 * j + 32, half, w, :, :])
                    ins.then_inc(p_s, 1)
                t = Tile(i, r + 2)
                if t.there():
                    pe.wait_ge(s_xin, 16 * (t.n + 1))
                    if not t.fixed or t.n >= 5:
                        pe.wait_ge(v_pos, t.n - 4)
                    if t.after(1):
                        pe.wait_ge(a_xn, t.n)
                    for k in range(2):
                        ins = pe.transpose(bank[0][:, k * CH:(k + 1) * CH], xin[:, k, :], ident[0:CH, 0:CH])
                    ins.then_inc(p_x, 1)
                t = Tile(i, r - 1)
                if t.there():
                    pe.wait_ge(g_norm, t.n + 1)
                    if t.after(1):
                        pe.wait_ge(a_pT, t.n)
                    if t.there(1):
                        pe.wait_ge(v_v, t.n + 2)
                    for j in range(NH // 2):
                        o = (pTa if j < 3 else pTb)[:, (j % 3) * P:(j % 3 + 1) * P]
                        ins = pe.transpose(o, prob[t.par][:, 2 * j:2 * j + 2, :], ident)
                    ins.then_inc(p_pT, 1)
                t = Tile(i, r - 2)
                if t.there():
                    pe.wait_ge(v_xl, t.n + 1)
                    for k in range(2):
                        ins = pe.transpose(bank[1][0:CH, k * P:(k + 1) * P], row[t.par][0][:, k * CH:(k + 1) * CH], ident)
                    ins.then_inc(p_xl, 1)
                t = Tile(i, r + 1)
                if t.there():
                    pe.wait_ge(a_xn, t.n + 1)
                    if t.after(1):
                        pe.wait_ge(a_qk, t.n)
                    for n, w_sb in enumerate((wq, wk)):
                        for half in range(2):
                            for k in range(2):
                                ins = mm(bank[2][0:CH, (2 * n + half) * P:(2 * n + half + 1) * P],
                                         w_sb[:, k, half * CH:(half + 1) * CH], xnT[:, k, :], start=k == 0, stop=k == 1)
                    ins.then_inc(p_qk, 1)
                t = Tile(i, r - 1)
                if t.there():
                    pe.wait_ge(a_pT, t.n + 1)
                    pe.wait_ge(v_v, t.n + 1)
                    if t.after(1):
                        pe.wait_ge(a_xl, t.n)
                    for j in range(NH // 2):
                        for w in range(2):
                            ins = mm(bank[1][32 * (j % PAIRS):32 * (j % PAIRS) + 32,
                                             (j // PAIRS) * P + w * L:(j // PAIRS) * P + (w + 1) * L],
                                     vbd[t.par][:, w, j, :], pT[:, j, w * L:(w + 1) * L])
                    ins.then_inc(p_o, 1)
                t = Tile(i, r + 1)
                if t.there():
                    if t.after(2):
                        pe.wait_ge(a_pT, t.n - 1)
                    elif t.n == 1:
                        pe.wait_ge(v_v, 1)
                    for k in range(2):
                        ins = mm(bank[3][:, 0:C], xnT[:, k, :], wv[:, k, :], start=k == 0, stop=k == 1)
                    ins.then_inc(p_v, 1)
                t = Tile(i, r - 2)
                if t.there():
                    pe.wait_ge(a_xl, t.n + 1)
                    if t.there(4):
                        pe.wait_ge(v_x, t.n + 5)
                    elif t.after(1):
                        pe.wait_ge(v_pos, t.n)
                    for k in range(2):
                        ins = mm(bank[0][:, 0:E], xlT[0:CH + k, k, :], gw[0:CH + k, k, :], start=k == 0, stop=k == 1)
                    ins.then_inc(p_gate, 1)
                t = Tile(i, r + 2)
                if t.there():
                    pe.wait_ge(v_xn, t.n + 1)
                    if not t.fixed or t.n >= 4:
                        pe.wait_ge(v_sc, t.n - 3)
                    for k in range(2):
                        ins = pe.transpose(bank[0][0:CH, k * P:(k + 1) * P], xn[:, k * CH:(k + 1) * CH], ident)
                    ins.then_inc(p_xn, 1)
                t = Tile(i, r - 1)
                if t.there():
                    pe.wait_ge(a_o, t.n + 1)
                    for k in range(2):
                        ins = mm(bank[1][:, 0:C], oT[0:CH + k, k, :], wo[0:CH + k, k, :], start=k == 0, stop=k == 1)
                    ins.then_inc(p_y, 1)
                t = Tile(i, r - 2)
                if t.there():
                    pe.wait_ge(v_cnt, t.n + 1)
                    if t.there(4):
                        pe.wait_ge(a_xn, t.n + 5)
                    if t.after(1):
                        pe.wait_ge(v_seen, t.n)
                    mm(bank[0][:, 0:E], before, cnt[t.par][:, :], stop=False)
                    mm(bank[0][:, 0:E], ones[:, :], seen[:, :], start=False).then_inc(p_pos, 1)

            for s in range(FIRST, 2 * LOOP_A):
                slot_(s // 2, s % 2)
            with pe.Fori(LOOP_A, LOOP_B) as i:
                slot_(i, 0)
                slot_(i, 1)
            for s in range(2 * LOOP_B, LAST):
                slot_(s // 2, s % 2)
            pe.wait_ge(v_seen, NT)
            pe.wait_ge(v_pos, NT)
            mm(bank[0][:, 0:E], ones[:, :], seen[:, :]).then_inc(p_tot, 1)

            def expert(b):
                return pe.value_load(exp_i[0:1, bass.ds(b, 1)], min_val=0, max_val=E - 1)

            def rows_in(b, par, done):
                pe.wait_ge(s_rowin[par], done)
                if not isinstance(b, int) or b >= 1:
                    pe.wait_ge(v_bx, b)
                for k in range(2):
                    ins = pe.transpose(bank[0][0:CH, k * P:(k + 1) * P], rowin[par][:, k * CH:(k + 1) * CH], ident)
                ins.then_inc(p_bx, 1)

            def up(b, e):
                pe.wait_ge(v_bx, b + 1)
                if not isinstance(b, int) or b >= 1:
                    pe.wait_ge(a_gelu, b)
                for n in range(2):
                    o = up_ps[:, n, 0:HW_F]
                    for k in range(2):
                        at = e * (2 * F) + (k * F + n * HW_F)
                        wh = w1h[0:CH + 2 * k, :, :].rearrange("p a f -> p (a f)")[:, bass.ds(at, HW_F)]
                        whx = w1h[0:CH, :, :].rearrange("p a f -> p (a f)")[:, bass.ds(at, HW_F)]
                        wl = w1l[0:CH, :, :].rearrange("p a f -> p (a f)")[:, bass.ds(at, HW_F)]
                        mm(o, xTh[0:CH + 2 * k, k, :], wh, start=k == 0, stop=False)
                        mm(o, xTh[0:CH, k, :], wl, start=False, stop=False)
                        ins = mm(o, xTl[0:CH, k, :], whx, start=False, stop=k == 1)
                ins.then_inc(p_up, 1)

            def hidT(b):
                pe.wait_ge(a_gelu, b + 1)
                if not isinstance(b, int) or b >= 1:
                    pe.wait_ge(v_lo, 2 * b)
                for f in range(FT):
                    ins = pe.transpose(up_ps[:, 2 + f // 3, (f % 3) * P:(f % 3 + 1) * P], hid[:, f * P:(f + 1) * P], ident)
                ins.then_inc(p_hT, 1)

            def down(b, e):
                if not isinstance(b, int) or b >= 1:
                    pe.wait_ge(v_yrow, b)
                at2 = e * (FT * 2 * C)
                w2f = w2s[:, :, :].rearrange("p a c -> p (a c)")
                for f in range(FT):
                    if f % 3 == 0:
                        pe.wait_ge(v_lo, 2 * b + f // 3 + 1)
                    mm(bank[1][:, 0:2 * C], hTh[:, f, :], w2f[:, bass.ds(at2 + f * 2 * C, 2 * C)], start=f == 0, stop=False)
                    mm(bank[1][:, 0:C], hTl[:, f, :], w2f[:, bass.ds(at2 + f * 2 * C, C)], start=False, stop=False)
                mm(bank[1][:, 0:C], ones2[:, :], b2r[:, bass.ds(e * C, C)], start=False, stop=True).then_inc(p_dn, 1)

            pe.wait_ge(v_tab, 12)
            pe.wait_ge(s_lo, NCH)
            pe.wait_ge(s_b1, NCH // 2)
            pe.wait_ge(s_b2, 2)
            e_now = expert(0)
            rows_in(0, 0, 16)
            up(0, e_now)
            rows_in(1, 1, 16)

            def blk(b, par, nxt, done):
                hidT(b)
                if nxt >= 1:
                    up(b + 1, expert(b + 1))
                if nxt >= 2:
                    rows_in(b + 2, par, done)
                down(b, expert(b))

            blk(0, 0, 2, 32)
            blk(1, 1, 2, 32)
            with pe.Fori(1, (NBLK - 2) // 2) as i:
                blk(2 * i, 0, 2, 16 * i + 32)
                blk(2 * i + 1, 1, 2, 16 * i + 32)
            for b in range((NBLK - 2) // 2 * 2, NBLK):
                blk(b, b % 2, min(2, NBLK - 1 - b), 16 * (b // 2) + 32)

            for t in range(NT):
                pe.wait_ge(v_z, t + 1)
                if t >= 2:
                    pe.wait_ge(a_z, t - 1)
                for k in range(2):
                    ins = pe.transpose(bank[2 + t % 2][0:CH, k * P:(k + 1) * P], z[t % 2][:, k * CH:(k + 1) * CH], ident)
                ins.then_inc(p_z, 1)


_OUT = ((B, C, IMG, IMG), "float32")


def kernel(x, L0_conv_Wq, L0_conv_Wk, L0_conv_Wv, L0_conv_Wo_w, L0_conv_Wo_b, L0_conv_rel_pos_bias,
           L0_conv_rel_coords, L0_ffn_gate_w, L0_ffn_gate_b, L0_ffn_w1, L0_ffn_b1, L0_ffn_w2, L0_ffn_b2):
    import concourse.bacc as _bacc
    from concourse.bass_utils import run_bass_kernel_spmd as _run

    c, places = constants()
    arrays = {
        "x": x, "wqT": np.asarray(L0_conv_Wq).T, "wkT": np.asarray(L0_conv_Wk).T, "wvT": np.asarray(L0_conv_Wv).T,
        "woT": np.asarray(L0_conv_Wo_w).T, "wo_b": L0_conv_Wo_b, "relT": np.asarray(L0_conv_rel_pos_bias).T,
        "coords": np.asarray(L0_conv_rel_coords).reshape(-1), "gate_w": L0_ffn_gate_w, "gate_b": L0_ffn_gate_b,
        "w1": L0_ffn_w1, "b1": L0_ffn_b1, "w2": L0_ffn_w2, "b2": L0_ffn_b2, "const_d": c, "place_d": places,
    }
    arrays = {f"in_{n}": np.ascontiguousarray(a) for n, a in arrays.items()}
    nc = _bacc.Bacc("TRN2", target_bir_lowering=False, num_devices=1)
    args = [nc.dram_tensor(n, a.shape, mybir.dt.from_np(a.dtype), kind="ExternalInput").ap() for n, a in arrays.items()]
    args.append(nc.dram_tensor("out_0", _OUT[0], mybir.dt.from_np(np.dtype(_OUT[1])), kind="ExternalOutput").ap())
    program(nc, *args)
    r = _run(nc, [arrays], core_ids=[0])
    return r.results[0]["out_0"]
```

```python
import concourse.bass as bass
from concourse import mybir
from contextlib import ExitStack
import numpy as np

B, C, IMG = 8, 192, 16
WIN = 8
L = WIN * WIN
NH, HD = 12, 16
P = 128
N = B * IMG * IMG
NT = N // P
CH = C // 2
PAIRS = CH // (2 * HD)
E, F = 6, 768
FT = F // P
NREL = (2 * WIN - 1) ** 2
CAP = N + P
PADROW = E * CAP
NBLK = (2 * N + E * (P - 1)) // P
ROW = C + 2
SKIP = 1 << 20
NCH = 2 * E
HW_F = F // 2
RC = 512
NSTEP = L * L // RC
NLOAD = 10

_at = {}
_n = 0
for _name, _w in (("ident", P), ("before", P), ("parity", 2), ("experts", 2 * E), ("region", E),
                  ("relrow", 2), ("twice", P)):
    _at[_name] = (_n, _n + _w)
    _n += _w
NCONST = _n


def constants():
    c = np.zeros((P, NCONST), np.float32)
    p = np.arange(P)

    def put(name, v):
        a, b = _at[name]
        c[:, a:b] = v

    put("ident", np.eye(P))
    put("before", p[:, None] < p[None, :])
    put("parity", (p[:, None] // HD) % 2 == np.arange(2)[None, :])
    put("experts", np.tile(np.arange(E), 2)[None, :])
    put("region", (np.arange(E) * CAP)[None, :])
    put("relrow", p[:, None] + P * np.arange(2)[None, :])
    put("twice", p[:, None] % L == p[None, :] % L)
    table = np.concatenate([np.repeat(np.arange(NBLK), E), (np.arange(E)[None, :] <= np.arange(E)[:, None]).reshape(-1),
                            np.arange(NBLK) * P]).astype(np.float32)[None, :]
    place = p[:, None, None] + P * np.arange(NT)[None, :, None] + N * np.arange(2)[None, None, :]
    places = np.concatenate([place.reshape(P, 2 * NT), np.full((P, 1), SKIP)], 1).astype(np.int32)
    return c, table, places


def program(nc, x, wqT, wkT, wvT, woT, wo_b, relT, coords, gate_w, gate_b, w1, b1, w2, b2,
            const_d, table_d, place_d, out):
    f32, f32r, i32, u32 = mybir.dt.float32, mybir.dt.float32r, mybir.dt.int32, mybir.dt.uint32
    bf16 = mybir.dt.bfloat16
    ALU, ACT, AX = mybir.AluOpType, mybir.ActivationFunctionType, mybir.AxisListType
    NEG = -3.0e38

    bias_d = nc.dram_tensor("bias_d", [NH, L * L], f32, kind="Internal").ap()
    routed = nc.dram_tensor("routed", [PADROW + P, ROW], f32, kind="Internal").ap()
    made = nc.dram_tensor("made", [2 * N, C], f32, kind="Internal").ap()

    with ExitStack() as ctx:
        def sb(name, shape, dt=f32):
            return ctx.enter_context(nc.sbuf_tensor(name, shape, dt))

        def sem(name):
            return ctx.enter_context(nc.semaphore(name))

        cst = sb("cst", [P, NCONST])
        places = sb("places", [P, 2 * NT + 1], i32)
        wq, wk, wv = (sb(n, [CH, 2, C]) for n in ("wq", "wk", "wv"))
        wo = sb("wo", [CH + 1, 2, C])
        gw = sb("gw", [CH + 1, 2, E])
        w1h = sb("w1h", [CH + 2, NCH, F], f32r)
        w1l = sb("w1l", [CH, NCH, F], f32r)
        w2s = sb("w2s", [P, E * FT, 2 * C], f32r)
        b2r = sb("b2r", [2, E * C], f32r)
        raw1 = [sb(f"raw1_{n}", [CH, F]) for n in range(2)]
        raw2 = [sb(f"raw2_{n}", [P, FT // 2, C]) for n in range(2)]
        bias = sb("bias", [P, NH, L])
        ones = sb("ones", [P, P], bf16)
        earlier = sb("earlier", [P, P], bf16)
        ones2 = sb("ones2", [2, P], f32r)
        arena = sb("arena", [P, 4 * RC])
        crd = [arena[:, n * RC:(n + 1) * RC].bitcast(i32) for n in range(2)]
        bT = [arena[0:NH, (2 + n) * RC:(3 + n) * RC] for n in range(2)]
        back = [arena[:, n * 2 * C:(n + 1) * 2 * C].rearrange("p (k c) -> p k c", k=2) for n in range(4)]
        c_block = arena[0:1, 3 * RC:3 * RC + NBLK * E].rearrange("p (a b) -> p a b", a=NBLK)
        c_upto = arena[0:1, 3 * RC + NBLK * E:3 * RC + NBLK * E + E * E].rearrange("p (a b) -> p a b", a=E)
        c_row = arena[0:1, 3 * RC + (NBLK + E) * E:3 * RC + (NBLK + E) * E + NBLK]
        c_all = arena[0:1, 3 * RC:3 * RC + (NBLK + E) * E + NBLK]
        split = sb("split", [P, 4 * RC], f32r)
        hot = [split[:, n * 2 * RC:(n + 1) * 2 * RC].rearrange("p (k c) -> p k c", k=2) for n in range(2)]
        hTh = split[:, 0:F].rearrange("p (f t) -> p f t", f=FT)
        hTl = split[:, F:2 * F].rearrange("p (f t) -> p f t", f=FT)
        relraw = sb("relraw", [P, 2, NH])
        relh = sb("relh", [P, 2, NH], f32r)
        rell = sb("rell", [P, 2, NH], f32r)
        ytok = sb("ytok", [P, NT, C])
        n1, n2 = E * F // CH, E * C // CH
        b1raw, b2raw = ytok[0:CH, NT - 1, 0:n1], ytok[0:CH, NT - 1, n1:n1 + n2]
        b1parts = ytok[0:CH, NT - 1, n1 + n2:3 * n1 + n2].bitcast(f32r).rearrange("p (k n) -> p k n", k=2)
        b2parts = ytok[0:CH, NT - 1, 3 * n1 + n2:3 * n1 + 3 * n2].bitcast(f32r).rearrange("p (k n) -> p k n", k=2)
        xin = sb("xin", [CH, 2, P])
        xpad = sb("xpad", [P, ROW])
        xn = xpad[:, 0:C]
        xnT = sb("xnT", [CH, 2, P])
        qT = sb("qT", [CH, 2, P])
        kbd = sb("kbd", [CH, 2, 2, 2, L])
        vbd = [sb(f"vbd{n}", [P, 2, NH // 2, 2, HD + 1]) for n in range(2)]
        prob = [sb(f"prob{n}", [P, NH, L]) for n in range(2)]
        pT = sb("pT", [P, NH // 2, P])
        hid = pT[:, :, :].rearrange("p a b -> p (a b)")
        oT = sb("oT", [CH + 1, 2, P])
        rmax = sb("rmax", [P, NH])
        inv = sb("inv", [P, NH])
        osb = sb("osb", [P, C])
        st, st2 = sb("st", [P, 6]), sb("st2", [P, 6])
        mv, mv2 = sb("mv", [P, 2]), sb("mv2", [P, 2])
        veps, veps2, rstd, rstd2, half_neg = (sb(n, [P, 1]) for n in ("veps", "veps2", "rstd", "rstd2", "half_neg"))
        row = [[sb(f"row{n}{k}", [P, ROW]) for k in range(2)] for n in range(2)]
        rowin = [row[n][0] for n in range(2)]
        yrow = [row[n][1] for n in range(2)]
        xlT = sb("xlT", [CH + 1, 2, P])
        score = sb("score", [P, 8])
        top = sb("top", [P, 8])
        topi = sb("topi", [P, 8], u32)
        topf = sb("topf", [P, 2])
        pick = [sb(f"pick{n}", [P, 2, E]) for n in range(2)]
        cnt = [sb(f"cnt{n}", [P, E], bf16) for n in range(2)]
        seen = sb("seen", [P, E], bf16)
        slot_e = sb("slot_e", [P, E])
        slot_p = sb("slot_p", [P, 2, E])
        slot_f = sb("slot_f", [P, 2])
        slot = [sb(f"slot{n}", [P, 2], i32) for n in range(2)]
        tops = sb("tops", [P, NT, 2])
        gates = sb("gates", [P, 2, NT])
        gtmp = sb("gtmp", [P, NT])
        tot_i, nb_i, pad_i = (sb(n, [1, E], i32) for n in ("tot_i", "nb_i", "pad_i"))
        tot_f, nb_f, last_f, pad_f = (sb(n, [1, E]) for n in ("tot_f", "nb_f", "last_f", "pad_f"))
        tri = arena[0:1, 0:E * E].rearrange("p (a b) -> p a b", a=E)
        past, past_n = (arena[0:1, n * RC:n * RC + NBLK * E].rearrange("p (a b) -> p a b", a=NBLK) for n in (1, 2))
        exp_f, base_f, off_f = (sb(n, [1, NBLK]) for n in ("exp_f", "base_f", "off_f"))
        exp_i, off_i = (sb(n, [1, NBLK], i32) for n in ("exp_i", "off_i"))
        xTh, xTl = (split[0:CH + 2, 2 * F + n * 2 * P:2 * F + (n + 1) * 2 * P].rearrange("p (k t) -> p k t", k=2)
                    for n in range(2))
        ylow = prob[0][:, 6:9, :].rearrange("p a b -> p (a b)")
        ring = sb("ring", [P, NBLK], i32)
        dest = [sb(f"dest{n}", [P, 1], i32) for n in range(2)]
        z = [prob[n][:, 0:3, :].rearrange("p a b -> p (a b)") for n in range(2)]
        oc = [xnT, qT]

        bank = [ctx.enter_context(nc.psum_tensor(f"bank{n}", [P, 512], f32)) for n in range(4)]
        up_ps = ctx.enter_context(nc.psum_tensor("up_ps", [P, 4, 512], f32))
        s_ps = up_ps[:, 0:3, 0:2 * P]
        bank7 = up_ps[:, 3, :]
        pTa = bank7[:, 0:3 * P]
        pTb = bank[3][:, 0:3 * P]

        ident = cst[:, slice(*_at["ident"])]
        before = cst[:, slice(*_at["before"])]
        parity = cst[:, slice(*_at["parity"])]
        experts = cst[:, slice(*_at["experts"])].rearrange("p (k e) -> p k e", k=2)
        region = cst[:, slice(*_at["region"])]
        relrow = cst[:, slice(*_at["relrow"])]
        twice = cst[:, slice(*_at["twice"])]

        s_const, s_bload = sem("s_const"), sem("s_bload")
        s_crd = [sem("s_crd0"), sem("s_crd1")]
        s_xin = sem("s_xin")
        s_raw = [sem("s_raw0"), sem("s_raw1")]
        s_set, s_rel, s_apart = sem("s_set"), sem("s_rel"), sem("s_apart")
        s_parts, s_rows = sem("s_parts"), sem("s_rows")
        s_hot, s_bmm, s_bev, s_bias = (sem(n) for n in ("s_hot", "s_bmm", "s_bev", "s_bias"))
        s_bout = [sem("s_bout0"), sem("s_bout1")]
        s_hi, s_lo = sem("s_hi"), sem("s_lo")
        (p_x, p_xn, p_qk, p_v, p_s, p_pT, p_o, p_oT, p_y, p_xl, p_gate, p_pos) = (
            sem(n) for n in ("p_x", "p_xn", "p_qk", "p_v", "p_s", "p_pT", "p_o", "p_oT", "p_y", "p_xl", "p_gate", "p_pos"))
        a_qk, a_exp, a_pT, a_xn, a_xl, a_row, a_o, a_v = (
            sem(n) for n in ("a_qk", "a_exp", "a_pT", "a_xn", "a_xl", "a_row", "a_o", "a_v"))
        v_max, v_sub, v_x, v_mv, v_xn, v_inv, v_o = (
            sem(n) for n in ("v_max", "v_sub", "v_x", "v_mv", "v_xn", "v_inv", "v_o"))
        v_sc, v_top, v_topi, v_topf, v_pick, v_cnt = (
            sem(n) for n in ("v_sc", "v_top", "v_topi", "v_topf", "v_pick", "v_cnt"))
        v_y, v_st2, v_mv2, v_xl, v_pos, v_sp, v_sf, v_slot, v_seen = (
            sem(n) for n in ("v_y", "v_st2", "v_mv2", "v_xl", "v_pos", "v_sp", "v_sf", "v_slot", "v_seen"))
        g_ve, g_rs, g_ve2, g_rs2, g_dst = (sem(n) for n in ("g_ve", "g_rs", "g_ve2", "g_rs2", "g_dst"))
        s_scat = [sem("s_scat0"), sem("s_scat1")]
        p_tot, v_tab, v_gate, a_gate, s_pad = (sem(n) for n in ("p_tot", "v_tab", "v_gate", "a_gate", "s_pad"))
        s_rowin = [sem("s_rowin0"), sem("s_rowin1")]
        p_bx, p_up, p_hT, p_dn = (sem(n) for n in ("p_bx", "p_up", "p_hT", "p_dn"))
        a_hi, a_gelu, a_ylow = (sem(n) for n in ("a_hi", "a_gelu", "a_ylow"))
        v_lo, v_bxh, v_bx, v_ring, v_yrow = (sem(n) for n in ("v_lo", "v_bxh", "v_bx", "v_ring", "v_yrow"))
        s_made = [sem("s_made0"), sem("s_made1")]
        s_back = [sem(f"s_back{n}") for n in range(4)]
        s_table = sem("s_table")
        v_z1, v_z, p_z, a_z = (sem(n) for n in ("v_z1", "v_z", "p_z", "a_z"))
        s_out = [sem("s_out0"), sem("s_out1")]

        FIRST, LAST = -2, NT + 2
        LOOP_A, LOOP_B = 2, NT // 2 - 1

        class Tile:

            def __init__(self, i, d):
                self.n, self.par, self.fixed = 2 * i + d, d % 2, isinstance(i, int)
                self.pair = i + d // 2

            def there(self, ahead=0):
                return not self.fixed or 0 <= self.n + ahead < NT

            def after(self, k):
                return not self.fixed or self.n >= k

        def wait_apart(eng, semaphore, value):
            eng.wait_ge(semaphore, value)
            eng.sem_inc(s_apart, 1)

        def windows(ap):
            return ap.rearrange("p (i w j) -> p w i j", i=WIN, w=2)

        def windowed(ap):
            return ap.rearrange("p (w i j) -> p w i j", w=2, i=WIN)

        w1_v = w1.rearrange("e (k p) f -> (e k) p f", p=CH)
        w2_v = w2.rearrange("e (k f p) n -> (e k) p f n", k=2, p=P)
        x_v = x.rearrange("b (k p) h w -> b p k (h w)", p=CH)
        out_v = out.rearrange("b (k p) h w -> b p k (h w)", p=CH)
        made_v = made.rearrange("(k t p) c -> t p k c", k=2, p=P)

        block = ctx.enter_context(nc.Block())

        @block.sync
        def _(sp):
            def load_x(t):
                if not t.there():
                    return
                if t.after(1):
                    sp.wait_ge(p_x, t.n)
                sp.dma_start(xin[:, :, :], x_v[bass.ds(t.pair, 1), :, :, t.par * P:(t.par + 1) * P]
                             .rearrange("b p k n -> (b p) k n")).then_inc(s_xin, 16)

            def load_chunk(i, r):
                c = 2 * i + r
                if isinstance(i, int) and not 0 <= c < NCH:
                    return
                if not isinstance(i, int) or c >= 2:
                    sp.wait_ge(s_lo, c - 1)
                sp.dma_start(raw1[r][:, :], w1_v[bass.ds(c, 1), :, :].rearrange("a p f -> (a p) f")).then_inc(s_raw[r], 16)
                sp.dma_start(raw2[r][:, :, :], w2_v[bass.ds(c, 1), :, :, :].rearrange("a p f n -> (a p) f n")).then_inc(s_raw[r], 16)

            load_x(Tile(0, 0))
            for n in range(2):
                sp.dma_start(crd[n], coords[n * RC:(n + 1) * RC].partition_broadcast(P)).then_inc(s_crd[n], 16)
            for n in range(2, NSTEP):
                sp.wait_ge(s_hot, n - 1)
                sp.dma_start(crd[n % 2], coords[n * RC:(n + 1) * RC].partition_broadcast(P)).then_inc(s_crd[n % 2], 16)
                if n == NSTEP // 2 + 1:
                    load_x(Tile(0, 1))
            sp.wait_ge(s_parts, 2)
            for k in range(2):
                for e in range(E):
                    sp.dma_start(w1h[CH + k:CH + k + 1, 2 * e + 1, :].bitcast(f32),
                                 b1parts[e * CH // E:(e + 1) * CH // E, k, :].bitcast(f32)).then_inc(s_rows, 16)
                sp.dma_start(b2r[k:k + 1, :].bitcast(f32), b2parts[:, k, :].bitcast(f32)).then_inc(s_rows, 16)
            for n in range(2):
                sp.wait_ge(s_bout[n], 16 * (NSTEP // 2))
            for w in range(2):
                sp.dma_start(bias[w * L:(w + 1) * L, :, :], bias_d.rearrange("h (l m) -> l h m", l=L)).then_inc(s_bias, 16)

            def slot_(i, r):
                load_x(Tile(i, r + 3))
                load_chunk(i, r)

            for s in range(-1, 2 * LOOP_A):
                slot_(s // 2, s % 2)
            with sp.Fori(LOOP_A, NCH // 2) as i:
                slot_(i, 0)
                slot_(i, 1)
            for s in range(NCH, LAST):
                slot_(s // 2, s % 2)
            sp.wait_ge(s_hot, NSTEP)
            sp.dma_start(c_all, table_d).then_inc(s_table, 16)

            sp.wait_ge(v_tab, 13)
            sp.wait_ge(g_dst, 3)
            for e in range(E):
                at = sp.value_load(pad_i[0:1, e:e + 1], min_val=e * CAP, max_val=e * CAP + N)
                sp.dma_start(routed[bass.ds(at, P), :], xpad[:, :]).then_inc(s_pad, 16)
            sp.dma_start(routed[PADROW:PADROW + P, :], xpad[:, :]).then_inc(s_pad, 16)
            for n in range(2):
                sp.wait_ge(s_scat[n], 32 * (NT // 2))
            sp.wait_ge(s_pad, 16 * (E + 1))

            def load_rows(b, par):
                if not isinstance(b, int) or b >= 2:
                    sp.wait_ge(v_ring, b - 1)
                at = sp.value_load(off_i[0:1, bass.ds(b, 1)], min_val=0, max_val=PADROW)
                sp.dma_start(rowin[par][:, :], routed[bass.ds(at, P), :]).then_inc(s_rowin[par], 16)

            load_rows(0, 0)
            load_rows(1, 1)
            with sp.Fori(1, NBLK // 2) as i:
                load_rows(2 * i, 0)
                load_rows(2 * i + 1, 1)
            if NBLK % 2:
                load_rows(NBLK - 1, 0)

            for n in range(2):
                sp.wait_ge(s_made[n], 16 * ((NBLK + 1 - n) // 2))
            def load_back(t):
                sp.dma_start(back[t % 4], made_v[t, :, :, :]).then_inc(s_back[t % 4], 16)

            for t in range(4):
                load_back(t)
            for t in range(NT):
                if t + 3 < NT and t >= 1:
                    sp.wait_ge(v_z, t)
                    load_back(t + 3)
                sp.wait_ge(a_z, t + 1)
                sp.dma_start(out_v[t // 2, :, :, (t % 2) * P:(t % 2 + 1) * P], oc[t % 2][:, :, :]).then_inc(s_out[t % 2], 16)
            for y in range(2):
                sp.wait_ge(s_out[y], 16 * B)

        @block.gpsimd
        def _(pool):
            def rstd_of(t, ready, mv_, veps_, rstd_, g_v, g_r, eps):
                if not t.there():
                    return
                wait_apart(pool, ready, t.n + 1)
                pool.tensor_scalar(veps_[:, :], mv_[:, 1:2], eps, None, ALU.add).then_inc(g_v, 1)
                pool.wait_ge(g_v, t.n + 1)
                pool.tensor_tensor(rstd_[:, :], veps_[:, :], half_neg[:, :], ALU.pow).then_inc(g_r, 1)

            def slot_(i, r):
                rstd_of(Tile(i, r - 2), v_mv2, mv2, veps2, rstd2, g_ve2, g_rs2, 1e-5)
                rstd_of(Tile(i, r + 2), v_mv, mv, veps, rstd, g_ve, g_rs, 1e-6)
                c = 2 * i + r - 1
                if not isinstance(i, int) or 0 <= c < NCH:
                    pool.wait_ge(s_hi, c + 1)
                    pool.tensor_tensor(w1l[:, bass.ds(c, 1), :].rearrange("p a f -> p (a f)"), raw1[1 - r][:, :],
                                       w1h[0:CH, bass.ds(c, 1), :].rearrange("p a f -> p (a f)").bitcast(f32), ALU.subtract)
                    pool.tensor_tensor(w2s[:, bass.ds(c * (FT // 2), FT // 2), C:2 * C], raw2[1 - r][:, :, :],
                                       w2s[:, bass.ds(c * (FT // 2), FT // 2), 0:C].bitcast(f32),
                                       ALU.subtract).then_inc(s_lo, 1)
                t = Tile(i, r - 3)
                if t.there():
                    pool.wait_ge(a_row, t.n + 1)
                    wait_apart(pool, v_slot, t.n + 1)
                    for k in range(2):
                        pool.indirect_dma_start(
                            out=routed[:, :], out_offset=bass.IndirectOffsetOnAxis(ap=slot[t.par][:, k:k + 1], axis=0),
                            in_=row[t.par][k][:, :], in_offset=None).then_inc(s_scat[t.par], 16)

            pool.wait_ge(s_set, 1)
            for s in range(FIRST, 2 * LOOP_A):
                slot_(s // 2, s % 2)
            with pool.Fori(LOOP_A, NCH // 2) as i:
                slot_(i, 0)
                slot_(i, 1)
            for s in range(NCH, LAST + 1):
                slot_(s // 2, s % 2)
            pool.wait_ge(p_xn, NT)
            pool.memset(xpad[:, :], 0.0).then_inc(g_dst, 1)
            pool.wait_ge(g_dst, 1)
            pool.tensor_copy(xpad[:, C:C + 1].bitcast(i32), places[:, 2 * NT:2 * NT + 1]).then_inc(g_dst, 2)

            bound = pool.to_reg(2 * N - 1)

            def store_rows(b, par):
                wait_apart(pool, v_yrow, b + 1)
                pool.indirect_dma_start(
                    out=made[:, :], out_offset=bass.IndirectOffsetOnAxis(ap=dest[par][:, :], axis=0),
                    in_=yrow[par][:, 0:C], in_offset=None, bounds_check=bound, oob_is_err=False).then_inc(s_made[par], 16)

            with pool.Fori(0, NBLK // 2) as i:
                store_rows(2 * i, 0)
                store_rows(2 * i + 1, 1)
            if NBLK % 2:
                store_rows(NBLK - 1, 0)

        @block.scalar
        def _(act):
            act.dma_start(cst[:, :], const_d).then_inc(s_const, 16)
            act.dma_start(places[:, :], place_d).then_inc(s_const, 16)
            act.dma_start(relraw[:, 0, :], relT[0:P, :]).then_inc(s_const, 16)
            act.dma_start(relraw[0:NREL - P, 1, :], relT[P:NREL, :]).then_inc(s_bload, 16)
            for w_sb, w_dr in ((wq, wqT), (wk, wkT), (wv, wvT), (wo, woT), (gw, gate_w)):
                act.dma_start(w_sb[0:CH, :, :], w_dr.rearrange("(k p) n -> p k n", p=CH)).then_inc(s_bload, 16)
            act.dma_start(wo[CH:CH + 1, 1, :], wo_b.unsqueeze(0)).then_inc(s_bload, 16)
            act.dma_start(gw[CH:CH + 1, 1, :], gate_b.unsqueeze(0)).then_inc(s_bload, 16)
            act.dma_start(b1raw, b1.rearrange("e f -> (e f)").rearrange("(p n) -> p n", p=CH)).then_inc(s_bload, 16)
            act.dma_start(b2raw, b2.rearrange("e n -> (e n)").rearrange("(p n) -> p n", p=CH)).then_inc(s_bload, 16)

            def bias_out(n):
                act.wait_ge(s_bmm, n + 1)
                if n >= 2:
                    act.wait_ge(s_bout[n % 2], 16 * (n // 2))
                act.activation(bT[n % 2], bank[2 + n % 2][0:NH, :], ACT.Copy).then_inc(s_bev, 1)
                act.wait_ge(s_bev, n + 1)
                act.dma_start(bias_d[:, n * RC:(n + 1) * RC], bT[n % 2]).then_inc(s_bout[n % 2], 16)

            for n in range(NSTEP // 2):
                bias_out(n)

            def slot_(i, r):
                t = Tile(i, r - 1)
                if t.there():
                    act.wait_ge(p_pT, t.n + 1)
                    if t.after(1):
                        act.wait_ge(p_o, t.n)
                    act.activation(pT[:, 0:3, :], pTa.rearrange("p (a b) -> p a b", a=3), ACT.Copy)
                    act.activation(pT[:, 3:6, :], pTb.rearrange("p (a b) -> p a b", a=3), ACT.Copy).then_inc(a_pT, 1)
                t = Tile(i, r - 2)
                if t.there():
                    act.wait_ge(p_xl, t.n + 1)
                    if t.after(1):
                        act.wait_ge(p_gate, t.n)
                    act.activation(xlT[0:CH, :, :], bank7[0:CH, 0:2 * P].rearrange("p (k n) -> p k n", k=2),
                                   ACT.Copy).then_inc(a_xl, 1)
                t = Tile(i, r)
                if t.there():
                    act.wait_ge(v_sub, t.n + 1)
                    p3 = prob[t.par][:, :, :]
                    act.activation(p3, p3, ACT.Exp).then_inc(a_exp, 1)
                t = Tile(i, r + 1)
                if t.there():
                    act.wait_ge(p_qk, t.n + 1)
                    if t.after(1):
                        act.wait_ge(p_s, t.n)
                    act.activation(qT[:, :, :], bank[2][0:CH, 0:2 * P].rearrange("p (k n) -> p k n", k=2),
                                   ACT.Copy, scale=float(HD) ** -0.5)
                    for h in range(2):
                        ins = act.activation(kbd[:, :, :, h, :],
                                             bank[2][0:CH, 2 * P:4 * P].rearrange("p (k w m) -> p k w m", k=2, w=2),
                                             ACT.Copy, scale=parity[0:CH, h:h + 1])
                    ins.then_inc(a_qk, 1)
                t = Tile(i, r - 1)
                if t.there():
                    act.wait_ge(p_oT, t.n + 1)
                    if t.after(1):
                        act.wait_ge(p_y, t.n)
                    for k in range(2):
                        ins = act.activation(windows(oT[0:CH, k, :]), windowed(bank[1][0:CH, k * P:(k + 1) * P]), ACT.Copy)
                    ins.then_inc(a_o, 1)
                t = Tile(i, r + 2)
                if t.there():
                    act.wait_ge(p_xn, t.n + 1)
                    if t.after(1):
                        act.wait_ge(p_v, t.n)
                    for k in range(2):
                        ins = act.activation(windowed(xnT[:, k, :]), windows(bank[0][0:CH, k * P:(k + 1) * P]), ACT.Copy)
                    ins.then_inc(a_xn, 1)
                t = Tile(i, r - 2)
                if t.there():
                    if t.after(2):
                        act.wait_ge(s_scat[t.par], 32 * t.pair)
                    act.activation(row[t.par][1][:, 0:C], row[t.par][0][:, 0:C], ACT.Copy).then_inc(a_row, 1)
                t = Tile(i, r + 1)
                if t.there():
                    act.wait_ge(p_v, t.n + 1)
                    if t.after(2):
                        act.wait_ge(p_o, t.n - 1)
                    for h in range(2):
                        for w in range(2):
                            ins = act.activation(
                                vbd[t.par][h * L:(h + 1) * L, w, :, h, 0:HD],
                                bank[3][w * L:(w + 1) * L, 0:C].rearrange("p (j h d) -> p j h d", h=2, d=HD)[:, :, h, :], ACT.Copy)
                    ins.then_inc(a_v, 1)
                c = 2 * i + r
                if not isinstance(i, int) or 0 <= c < NCH:
                    act.wait_ge(s_raw[r], 32 * (i + 1))
                    act.activation(w1h[0:CH, bass.ds(c, 1), :].rearrange("p a f -> p (a f)"), raw1[r][:, :], ACT.Copy)
                    act.activation(w2s[:, bass.ds(c * (FT // 2), FT // 2), 0:C], raw2[r][:, :, :],
                                   ACT.Copy).then_inc(s_hi, 1)

            slot_(-1, 0)
            for n in range(NSTEP // 2, NSTEP):
                bias_out(n)
            for s in range(FIRST + 1, 2 * LOOP_A):
                slot_(s // 2, s % 2)
            with act.Fori(LOOP_A, NCH // 2) as i:
                slot_(i, 0)
                slot_(i, 1)
            for s in range(NCH, LAST):
                slot_(s // 2, s % 2)
            act.wait_ge(v_gate, 1)
            act.activation(gates[:, 1, :], gtmp[:, :], ACT.Exp).then_inc(a_gate, 1)

            def gelu(b):
                act.wait_ge(p_up, b + 1)
                if not isinstance(b, int) or b >= 1:
                    act.wait_ge(p_hT, b)
                act.activation(hid.rearrange("p (n c) -> p n c", n=2), up_ps[:, 0:2, 0:HW_F], ACT.Gelu).then_inc(a_gelu, 1)

            def hi(b):
                act.wait_ge(p_hT, b + 1)
                if not isinstance(b, int) or b >= 1:
                    act.wait_ge(p_dn, b)
                for n in range(2):
                    act.activation(hTh[:, 3 * n:3 * n + 3, :], up_ps[:, 2 + n, 0:3 * P].rearrange("p (a b) -> p a b", a=3),
                                   ACT.Copy).then_inc(a_hi, 1)

            def ylow_(b):
                act.wait_ge(p_dn, b + 1)
                if not isinstance(b, int) or b >= 1:
                    act.wait_ge(v_yrow, b)
                act.activation(ylow[:, :], bank[1][:, C:2 * C], ACT.Copy).then_inc(a_ylow, 1)

            gelu(0)
            hi(0)
            gelu(1)
            ylow_(0)
            with act.Fori(1, NBLK - 1) as b:
                hi(b)
                gelu(b + 1)
                ylow_(b)
            hi(NBLK - 1)
            ylow_(NBLK - 1)

            def last(t, par):
                act.wait_ge(p_z, t + 1)
                if not isinstance(t, int) or t >= 2:
                    act.wait_ge(s_out[par], 16 * (t // 2 if isinstance(t, int) else t_pair(t)))
                act.activation(oc[par][:, :, :], bank[2 + par][0:CH, 0:2 * P].rearrange("p (k n) -> p k n", k=2),
                               ACT.Copy).then_inc(a_z, 1)

            pair_of = {}

            def t_pair(t):
                return pair_of["i"]

            last(0, 0)
            last(1, 1)
            with act.Fori(1, NT // 2) as i:
                pair_of["i"] = i
                last(2 * i, 0)
                last(2 * i + 1, 1)

        @block.vector
        def _(dve):
            dve.memset(ones[:, :], 1.0)
            dve.memset(ones2[:, :].bitcast(f32), 1.0)
            dve.memset(oT[CH:CH + 1, :, :], 1.0)
            dve.memset(xlT[CH:CH + 1, :, :], 1.0)
            dve.memset(half_neg[:, :], -0.5)
            for n in range(2):
                dve.memset(vbd[n][:, :, :, :, :], 0.0)
                for k in range(2):
                    dve.memset(row[n][k][:, C:ROW], 0.0)
            dve.memset(score[:, :], NEG)
            dve.memset(seen[:, :], 0.0).then_inc(s_set, 1)
            dve.wait_ge(s_set, 1)
            for n in range(2):
                for h in range(2):
                    ins = dve.memset(vbd[n][h * L:(h + 1) * L, :, :, h, HD], 1.0)
            ins.then_inc(s_set, 1)
            dve.wait_ge(s_const, 16 * 3)
            dve.wait_ge(s_bload, 16 * NLOAD)
            dve.tensor_copy(earlier[:, :], before)
            dve.tensor_copy(relh[:, 0, :], relraw[:, 0, :])
            dve.tensor_copy(relh[0:NREL - P, 1, :], relraw[0:NREL - P, 1, :])
            for raw, parts in ((b1raw, b1parts), (b2raw, b2parts)):
                ins = dve.tensor_copy(parts[:, 0, :], raw)
            ins.then_inc(s_parts, 1)
            dve.wait_ge(s_parts, 1)
            dve.tensor_tensor(rell[:, 0, :], relraw[:, 0, :], relh[:, 0, :].bitcast(f32), ALU.subtract)
            dve.tensor_tensor(rell[0:NREL - P, 1, :], relraw[0:NREL - P, 1, :],
                              relh[0:NREL - P, 1, :].bitcast(f32), ALU.subtract).then_inc(s_rel, 1)
            for raw, parts in ((b1raw, b1parts), (b2raw, b2parts)):
                ins = dve.tensor_tensor(parts[:, 1, :], raw, parts[:, 0, :].bitcast(f32), ALU.subtract)
            ins.then_inc(s_parts, 1)

            def one_hots(n):
                dve.wait_ge(s_crd[n % 2], 16 * (n // 2 + 1))
                if n >= 2:
                    dve.wait_ge(s_bmm, n - 1)
                for k in range(2):
                    ins = dve.tensor_scalar(hot[n % 2][:, k, :], crd[n % 2], relrow[:, k:k + 1], None, ALU.is_equal)
                ins.then_inc(s_hot, 1)

            def slot_(i, r):
                t = Tile(i, r + 2)
                if t.there():
                    dve.wait_ge(p_x, t.n + 1)
                    dve.tensor_copy(ytok[:, bass.ds(t.n, 1), :].rearrange("p a c -> p (a c)"), bank[0][:, 0:C])
                    if t.after(1):
                        wait_apart(dve, v_mv, t.n)
                    dve.bn_stats(st[:, :], bank[0][:, 0:C]).then_inc(v_x, 1)
                    if t.after(1):
                        dve.wait_ge(g_ve, t.n)
                        dve.wait_ge(v_xn, t.n)
                    wait_apart(dve, v_x, t.n + 1)
                    dve.bn_aggr(mv[:, :], st[:, :]).then_inc(v_mv, 1)
                t = Tile(i, r - 2)
                if t.there():
                    dve.wait_ge(g_rs2, t.n + 1)
                    if t.after(2):
                        dve.wait_ge(s_scat[t.par], 32 * t.pair)
                    dve.tensor_scalar(row[t.par][0][:, 0:C], ytok[:, bass.ds(t.n, 1), :].rearrange("p a c -> p (a c)"),
                                      mv2[:, 0:1], rstd2[:, 0:1], ALU.subtract, ALU.mult).then_inc(v_xl, 1)
                t = Tile(i, r)
                if t.there():
                    dve.wait_ge(p_s, t.n + 1)
                    if t.after(1):
                        dve.wait_ge(v_sub, t.n)
                    for k in range(2):
                        ins = dve.tensor_reduce(rmax[:, 6 * k:6 * k + 6].rearrange("p (j h) -> p j h", j=PAIRS),
                                                s_ps[:, :, k * P:(k + 1) * P].rearrange("p j (h m) -> p j h m", h=2),
                                                AX.X, ALU.max)
                    ins.then_inc(v_max, 1)
                    dve.wait_ge(v_max, t.n + 1)
                    if t.after(2):
                        dve.wait_ge(p_pT, t.n - 1)
                    for k in range(2):
                        for h in range(2):
                            ins = dve.tensor_tensor(
                                prob[t.par][:, 6 * k:6 * k + 6, :].rearrange("p (j h) m -> p j h m", j=PAIRS)[:, :, h, :],
                                s_ps[:, :, k * P + h * L:k * P + (h + 1) * L],
                                rmax[:, 6 * k:6 * k + 6].rearrange("p (j h) -> p j h", j=PAIRS)[:, :, h]
                                .unsqueeze(2).to_broadcast([P, PAIRS, L]), ALU.subtract)
                    ins.then_inc(v_sub, 1)
                t = Tile(i, r - 1)
                if t.there():
                    dve.wait_ge(p_o, t.n + 1)
                    if t.after(1):
                        dve.wait_ge(v_o, t.n)
                    o3 = bank[1][:, 0:NH * (HD + 1)].rearrange("p (h d) -> p h d", h=NH)
                    dve.reciprocal(inv[:, :], o3[:, :, HD]).then_inc(v_inv, 1)
                    dve.wait_ge(v_inv, t.n + 1)
                    if t.after(1):
                        dve.wait_ge(p_oT, t.n)
                    dve.tensor_tensor(osb[:, :].rearrange("p (h d) -> p h d", h=NH), o3[:, :, 0:HD],
                                      inv[:, :].unsqueeze(2).to_broadcast([P, NH, HD]), ALU.mult).then_inc(v_o, 1)
                t = Tile(i, r + 2)
                if t.there():
                    dve.wait_ge(g_rs, t.n + 1)
                    if t.after(1):
                        dve.wait_ge(p_xn, t.n)
                    dve.tensor_scalar(xn[:, :], ytok[:, bass.ds(t.n, 1), :].rearrange("p a c -> p (a c)"),
                                      mv[:, 0:1], rstd[:, 0:1], ALU.subtract, ALU.mult).then_inc(v_xn, 1)
                t = Tile(i, r - 3)
                if t.there():
                    dve.wait_ge(v_pos, t.n + 1)
                    if t.after(1):
                        dve.wait_ge(v_sf, t.n)
                    dve.tensor_tensor(slot_p[:, :, :], pick[t.par][:, :, :],
                                      slot_e[:, :].unsqueeze(1).to_broadcast([P, 2, E]), ALU.mult).then_inc(v_sp, 1)
                    for k in range(2):
                        dve.tensor_copy(row[t.par][k][:, C:C + 1].bitcast(i32), places[:, bass.ds(2 * t.n + k, 1)])
                    dve.wait_ge(v_sp, t.n + 1)
                    dve.tensor_reduce(slot_f[:, :], slot_p[:, :, :], AX.X, ALU.add).then_inc(v_sf, 1)
                    dve.wait_ge(v_sf, t.n + 1)
                    if t.after(2):
                        dve.wait_ge(s_scat[t.par], 32 * t.pair)
                    dve.tensor_copy(slot[t.par][:, :], slot_f[:, :]).then_inc(v_slot, 1)
                t = Tile(i, r - 2)
                if t.there():
                    dve.wait_ge(p_gate, t.n + 1)
                    if t.after(1):
                        dve.wait_ge(v_topi, t.n)
                    dve.tensor_copy(score[:, 0:E], bank7[:, 0:E]).then_inc(v_sc, 1)
                    wait_apart(dve, v_sc, t.n + 1)
                    dve.max(top[:, :], score[:, :]).then_inc(v_top, 1)
                    wait_apart(dve, v_top, t.n + 1)
                    dve.max_index(topi[:, :], top[:, :], score[:, :]).then_inc(v_topi, 1)
                    dve.tensor_copy(tops[:, bass.ds(t.n, 1), :].rearrange("p a k -> p (a k)"), top[:, 0:2])
                    dve.wait_ge(v_topi, t.n + 1)
                    dve.tensor_copy(topf[:, :], topi[:, 0:2]).then_inc(v_topf, 1)
                    dve.wait_ge(v_topf, t.n + 1)
                    dve.tensor_tensor(pick[t.par][:, :, :], experts, topf[:, :].unsqueeze(2).to_broadcast([P, 2, E]),
                                      ALU.is_equal).then_inc(v_pick, 1)
                    dve.wait_ge(v_pick, t.n + 1)
                    if t.after(2):
                        dve.wait_ge(v_seen, t.n - 1)
                        dve.wait_ge(p_pos, t.n - 1)
                    dve.tensor_tensor(cnt[t.par][:, :], pick[t.par][:, 0, :], pick[t.par][:, 1, :],
                                      ALU.add).then_inc(v_cnt, 1)
                t = Tile(i, r - 1)
                if t.there():
                    dve.wait_ge(p_y, t.n + 1)
                    yt = ytok[:, bass.ds(t.n, 1), :].rearrange("p a c -> p (a c)")
                    dve.tensor_tensor(yt, bank[1][:, 0:C], yt, ALU.add).then_inc(v_y, 1)
                    if t.after(1):
                        dve.wait_ge(v_mv2, t.n)
                    wait_apart(dve, v_y, t.n + 1)
                    dve.bn_stats(st2[:, :], yt).then_inc(v_st2, 1)
                    if t.after(1):
                        dve.wait_ge(g_ve2, t.n)
                        dve.wait_ge(v_xl, t.n)
                    wait_apart(dve, v_st2, t.n + 1)
                    dve.bn_aggr(mv2[:, :], st2[:, :]).then_inc(v_mv2, 1)
                t = Tile(i, r - 2)
                if t.there():
                    dve.wait_ge(p_pos, t.n + 1)
                    if t.after(1):
                        dve.wait_ge(v_sp, t.n)
                    dve.tensor_tensor(slot_e[:, :], bank7[:, 0:E], region, ALU.add).then_inc(v_pos, 1)
                    dve.tensor_tensor(seen[:, :], seen[:, :], cnt[t.par][:, :], ALU.add).then_inc(v_seen, 1)

            for n in range(NSTEP // 2):
                one_hots(n)
            slot_(-1, 0)
            for n in range(NSTEP // 2, NSTEP):
                one_hots(n)
            slot_(-1, 1)
            dve.wait_ge(s_rows, 16 * 2 * (E + 1))
            for s in range(0, 2 * LOOP_A):
                slot_(s // 2, s % 2)
            with dve.Fori(LOOP_A, NCH // 2) as i:
                slot_(i, 0)
                slot_(i, 1)
            for s in range(NCH, LAST + 1):
                slot_(s // 2, s % 2)

            step = [0]

            def then(ins):
                step[0] += 1
                ins.then_inc(v_tab, 1)
                dve.wait_ge(v_tab, step[0])

            dve.wait_ge(s_table, 16)
            dve.wait_ge(p_tot, 1)
            dve.tensor_tensor(pad_f[:, :], bank[0][0:1, 0:E], region[0:1, :], ALU.add)
            then(dve.tensor_scalar(tot_f[:, :], bank[0][0:1, 0:E], float(P - 1), None, ALU.add))
            dve.tensor_copy(pad_i[:, :], pad_f[:, :])
            then(dve.tensor_copy(tot_i[:, :], tot_f[:, :]))
            then(dve.tensor_scalar(nb_i[:, :], tot_i[:, :], 7, None, ALU.arith_shift_right))
            then(dve.tensor_copy(nb_f[:, :], nb_i[:, :]))
            nbb = nb_f[:, :].unsqueeze(1)
            then(dve.tensor_tensor(tri[:, :, :], c_upto,
                                   nbb.to_broadcast([1, E, E]), ALU.mult))
            then(dve.tensor_reduce(last_f[:, :], tri[:, :, :], AX.X, ALU.add))
            then(dve.tensor_tensor(past[:, :, :], c_block,
                                   last_f[:, :].unsqueeze(1).to_broadcast([1, NBLK, E]), ALU.is_ge))
            then(dve.tensor_tensor(past_n[:, :, :], past[:, :, :], nbb.to_broadcast([1, NBLK, E]), ALU.mult))
            dve.tensor_reduce(exp_f[:, :], past[:, :, :], AX.X, ALU.add)
            then(dve.tensor_reduce(base_f[:, :], past_n[:, :, :], AX.X, ALU.add))
            then(dve.scalar_tensor_tensor(out=off_f[:, :], in0=base_f[:, :], scalar=-float(P), in1=c_row,
                                          op0=ALU.mult, op1=ALU.add))
            then(dve.scalar_tensor_tensor(out=base_f[:, :], in0=exp_f[:, :], scalar=float(CAP), in1=off_f[:, :],
                                          op0=ALU.mult, op1=ALU.add))
            dve.tensor_scalar(off_i[:, :], base_f[:, :], float(PADROW), None, ALU.min)
            then(dve.tensor_scalar(exp_i[:, :], exp_f[:, :], float(E - 1), None, ALU.min))
            dve.tensor_tensor(gtmp[:, :], tops[:, :, 1], tops[:, :, 0], ALU.subtract).then_inc(v_gate, 1)
            dve.wait_ge(a_gate, 1)
            then(dve.tensor_scalar(gtmp[:, :], gates[:, 1, :], 1.0, None, ALU.add))
            dve.wait_ge(v_gate, 1)
            dve.reciprocal(gates[:, 0, :], gtmp[:, :]).then_inc(v_gate, 1)
            dve.wait_ge(v_gate, 2)
            dve.tensor_tensor(gates[:, 1, :], gates[:, 1, :], gates[:, 0, :], ALU.mult).then_inc(v_gate, 1)

            dve.memset(xTh[CH:CH + 2, :, :].bitcast(f32), 1.0)

            def x_parts(b, par):
                dve.wait_ge(p_bx, b + 1)
                if not isinstance(b, int) or b >= 1:
                    dve.wait_ge(p_up, b)
                xps = bank[0][0:CH, 0:2 * P].rearrange("p (k n) -> p k n", k=2)
                dve.tensor_copy(xTh[0:CH, :, :], xps).then_inc(v_bxh, 1)
                dve.tensor_copy(ring[:, bass.ds(b, 1)], rowin[par][:, C:C + 1].bitcast(i32)).then_inc(v_ring, 1)
                dve.wait_ge(v_bxh, b + 1)
                dve.tensor_tensor(xTl[0:CH, :, :], xps, xTh[0:CH, :, :].bitcast(f32), ALU.subtract).then_inc(v_bx, 1)

            def lo(b):
                for n in range(2):
                    dve.wait_ge(a_hi, 2 * b + n + 1)
                    dve.tensor_tensor(hTl[:, 3 * n:3 * n + 3, :], up_ps[:, 2 + n, 0:3 * P].rearrange("p (a b) -> p a b", a=3),
                                      hTh[:, 3 * n:3 * n + 3, :].bitcast(f32), ALU.subtract).then_inc(v_lo, 1)

            def y_out(b, par, turn):
                dve.wait_ge(a_ylow, b + 1)
                if not isinstance(b, int) or b >= 2:
                    dve.wait_ge(s_made[par], 16 * turn)
                dve.wait_ge(v_ring, b + 1)
                dve.tensor_copy(dest[par][:, :], ring[:, bass.ds(b, 1)])
                dve.tensor_tensor(yrow[par][:, 0:C], bank[1][:, 0:C], ylow[:, :], ALU.add).then_inc(v_yrow, 1)

            x_parts(0, 0)
            x_parts(1, 1)

            def blk(b, par, turn):
                lo(b)
                if not isinstance(b, int) or b + 2 < NBLK:
                    x_parts(b + 2, par)
                y_out(b, par, turn)

            blk(0, 0, 0)
            blk(1, 1, 0)
            with dve.Fori(1, (NBLK - 2) // 2) as i:
                blk(2 * i, 0, i)
                blk(2 * i + 1, 1, i)
            for b in range((NBLK - 2) // 2 * 2, NBLK):
                blk(b, b % 2, b // 2)

            def fin(t, par):
                dve.wait_ge(s_back[t % 4], 16 * (t // 4 + 1))
                if t >= 2:
                    dve.wait_ge(p_z, t - 1)
                dve.scalar_tensor_tensor(out=z[par], in0=back[t % 4][:, 0, :], scalar=gates[:, 0, t:t + 1],
                                         in1=ytok[:, t, :], op0=ALU.mult, op1=ALU.add).then_inc(v_z1, 1)
                dve.wait_ge(v_z1, t + 1)
                dve.scalar_tensor_tensor(out=z[par], in0=back[t % 4][:, 1, :], scalar=gates[:, 1, t:t + 1],
                                         in1=z[par], op0=ALU.mult, op1=ALU.add).then_inc(v_z, 1)

            dve.wait_ge(v_gate, 3)
            for t in range(NT):
                fin(t, t % 2)

        @block.tensor
        def _(pe):
            def mm(o, a, b_, start=True, stop=True):
                return pe.matmul(o, a, b_, start=start, stop=stop)

            def gather(n):
                pe.wait_ge(s_hot, n + 1)
                if n >= 2:
                    pe.wait_ge(s_bev, n - 1)
                for k, rows in ((0, P), (1, NREL - P)):
                    for part in (relh, rell):
                        ins = mm(bank[2 + n % 2][0:NH, :], part[0:rows, k, :], hot[n % 2][0:rows, k, :],
                                 start=(k == 0 and part is relh), stop=(k == 1 and part is rell))
                ins.then_inc(s_bmm, 1)

            def position(t, part):
                if not t.there():
                    return
                if t.fixed and t.n == 0:
                    pe.wait_ge(s_bias, 32)
                if t.after(1):
                    pe.wait_ge(v_sub, t.n)
                for j in part:
                    mm(s_ps[:, j, :], ident,
                       bias[:, :, :].rearrange("p (k j h) m -> p k j (h m)", k=2, j=PAIRS)[:, :, j, :])

            def slot_(i, r):
                t = Tile(i, r + 2)
                if t.there():
                    pe.wait_ge(s_xin, 16 * (t.n + 1))
                    if t.after(1):
                        pe.wait_ge(a_xn, t.n)
                    for k in range(2):
                        ins = pe.transpose(bank[0][:, k * CH:(k + 1) * CH], xin[:, k, :], ident[0:CH, 0:CH])
                    ins.then_inc(p_x, 1)
                t = Tile(i, r)
                if t.there():
                    pe.wait_ge(a_qk, t.n + 1)
                    for half in range(2):
                        for w in range(2):
                            for j in range(PAIRS):
                                ins = pe.matmul(s_ps[w * L:(w + 1) * L, j, half * P:(half + 1) * P],
                                                qT[32 * j:32 * j + 32, half, w * L:(w + 1) * L],
                                                kbd[32 * j:32 * j + 32, half, w, :, :], start=False, stop=True,
                                                skip_group_check=True)
                    ins.then_inc(p_s, 1)
                t = Tile(i, r - 1)
                if t.there():
                    pe.wait_ge(a_exp, t.n + 1)
                    if t.after(1):
                        pe.wait_ge(a_pT, t.n)
                    if t.after(2):
                        pe.wait_ge(v_pos, t.n - 1)
                    if t.there(1):
                        pe.wait_ge(a_v, t.n + 2)
                    for j in range(NH // 2):
                        o = (pTa if j < 3 else pTb)[:, (j % 3) * P:(j % 3 + 1) * P]
                        ins = pe.transpose(o, prob[t.par][:, 2 * j:2 * j + 2, :], ident)
                    ins.then_inc(p_pT, 1)
                t = Tile(i, r + 1)
                if t.there():
                    pe.wait_ge(a_xn, t.n + 1)
                    if t.after(1):
                        pe.wait_ge(a_qk, t.n)
                    for n, w_sb in enumerate((wq, wk)):
                        for half in range(2):
                            for k in range(2):
                                ins = mm(bank[2][0:CH, (2 * n + half) * P:(2 * n + half + 1) * P],
                                         w_sb[:, k, half * CH:(half + 1) * CH], xnT[:, k, :], start=k == 0, stop=k == 1)
                    ins.then_inc(p_qk, 1)
                t = Tile(i, r - 1)
                if t.there():
                    pe.wait_ge(a_pT, t.n + 1)
                    pe.wait_ge(a_v, t.n + 1)
                    if t.after(1):
                        pe.wait_ge(v_y, t.n)
                    for j in range(NH // 2):
                        for w in range(2):
                            ins = mm(bank[1][w * L:(w + 1) * L, j * 2 * (HD + 1):(j + 1) * 2 * (HD + 1)],
                                     pT[:, j, w * L:(w + 1) * L], vbd[t.par][:, w, j, :, :])
                    ins.then_inc(p_o, 1)
                t = Tile(i, r - 2)
                if t.there():
                    pe.wait_ge(v_xl, t.n + 1)
                    if t.there(1):
                        pe.wait_ge(a_pT, t.n + 2)
                    else:
                        pe.wait_ge(v_pos, t.n)
                    for k in range(2):
                        ins = pe.transpose(bank7[0:CH, k * P:(k + 1) * P], row[t.par][0][:, k * CH:(k + 1) * CH], ident)
                    ins.then_inc(p_xl, 1)
                t = Tile(i, r + 1)
                if t.there():
                    if t.after(2):
                        pe.wait_ge(a_pT, t.n - 1)
                    elif t.n == 1:
                        pe.wait_ge(a_v, 1)
                    for k in range(2):
                        ins = mm(bank[3][:, 0:C], xnT[:, k, :], wv[:, k, :], start=k == 0, stop=k == 1)
                    ins.then_inc(p_v, 1)
                position(Tile(i, r + 1), range(1))
                t = Tile(i, r - 1)
                if t.there():
                    pe.wait_ge(v_o, t.n + 1)
                    for k in range(2):
                        ins = pe.transpose(bank[1][0:CH, k * P:(k + 1) * P], osb[:, k * CH:(k + 1) * CH], ident)
                    ins.then_inc(p_oT, 1)
                t = Tile(i, r + 2)
                if t.there():
                    pe.wait_ge(v_xn, t.n + 1)
                    pe.wait_ge(v_x, t.n + 1)
                    for k in range(2):
                        ins = pe.transpose(bank[0][0:CH, k * P:(k + 1) * P], xn[:, k * CH:(k + 1) * CH], ident)
                    ins.then_inc(p_xn, 1)
                t = Tile(i, r - 2)
                if t.there():
                    pe.wait_ge(a_xl, t.n + 1)
                    for k in range(2):
                        ins = mm(bank7[:, 0:E], xlT[0:CH + k, k, :], gw[0:CH + k, k, :], start=k == 0, stop=k == 1)
                    ins.then_inc(p_gate, 1)
                position(Tile(i, r + 1), range(1, PAIRS))
                t = Tile(i, r - 1)
                if t.there():
                    pe.wait_ge(a_o, t.n + 1)
                    for k in range(2):
                        ins = mm(bank[1][:, 0:C], oT[0:CH + k, k, :], wo[0:CH + k, k, :], start=k == 0, stop=k == 1)
                    ins.then_inc(p_y, 1)
                t = Tile(i, r - 2)
                if t.there():
                    pe.wait_ge(v_cnt, t.n + 1)
                    if t.after(1):
                        pe.wait_ge(v_seen, t.n)
                    mm(bank7[:, 0:E], earlier[:, :], cnt[t.par][:, :], stop=False)
                    mm(bank7[:, 0:E], ones[:, :], seen[:, :], start=False).then_inc(p_pos, 1)

            pe.wait_ge(s_rel, 1)
            pe.wait_ge(s_set, 2)
            pe.wait_ge(s_bload, 16 * NLOAD)
            for n in range(NSTEP // 2):
                gather(n)
            slot_(-1, 0)
            for n in range(NSTEP // 2, NSTEP):
                gather(n)
            pe.wait_ge(s_bev, NSTEP)
            slot_(-1, 1)
            for s in range(0, 2 * LOOP_A):
                slot_(s // 2, s % 2)
            with pe.Fori(LOOP_A, LOOP_B) as i:
                slot_(i, 0)
                slot_(i, 1)
            for s in range(2 * LOOP_B, LAST):
                slot_(s // 2, s % 2)
            pe.wait_ge(v_seen, NT)
            mm(bank[0][:, 0:E], ones[:, :], seen[:, :]).then_inc(p_tot, 1)

            def expert(b):
                return pe.value_load(exp_i[0:1, bass.ds(b, 1)], min_val=0, max_val=E - 1)

            def rows_in(b, par, done):
                pe.wait_ge(s_rowin[par], done)
                if not isinstance(b, int) or b >= 1:
                    pe.wait_ge(v_bx, b)
                for k in range(2):
                    ins = pe.transpose(bank[0][0:CH, k * P:(k + 1) * P], rowin[par][:, k * CH:(k + 1) * CH], ident)
                ins.then_inc(p_bx, 1)

            def up(b, e):
                pe.wait_ge(v_bx, b + 1)
                if not isinstance(b, int) or b >= 1:
                    pe.wait_ge(a_gelu, b)
                for n in range(2):
                    o = up_ps[:, n, 0:HW_F]
                    for k in range(2):
                        at = e * (2 * F) + (k * F + n * HW_F)
                        wh = w1h[0:CH + 2 * k, :, :].rearrange("p a f -> p (a f)")[:, bass.ds(at, HW_F)]
                        whx = w1h[0:CH, :, :].rearrange("p a f -> p (a f)")[:, bass.ds(at, HW_F)]
                        wl = w1l[0:CH, :, :].rearrange("p a f -> p (a f)")[:, bass.ds(at, HW_F)]
                        mm(o, xTh[0:CH + 2 * k, k, :], wh, start=k == 0, stop=False)
                        mm(o, xTh[0:CH, k, :], wl, start=False, stop=False)
                        ins = mm(o, xTl[0:CH, k, :], whx, start=False, stop=k == 1)
                ins.then_inc(p_up, 1)

            def hidT(b):
                pe.wait_ge(a_gelu, b + 1)
                if not isinstance(b, int) or b >= 1:
                    pe.wait_ge(v_lo, 2 * b)
                for f in range(FT):
                    ins = pe.transpose(up_ps[:, 2 + f // 3, (f % 3) * P:(f % 3 + 1) * P], hid[:, f * P:(f + 1) * P], ident)
                ins.then_inc(p_hT, 1)

            def down(b, e):
                if not isinstance(b, int) or b >= 1:
                    pe.wait_ge(v_yrow, b)
                at2 = e * (FT * 2 * C)
                w2f = w2s[:, :, :].rearrange("p a c -> p (a c)")
                for f in range(FT):
                    if f % 3 == 0:
                        pe.wait_ge(v_lo, 2 * b + f // 3 + 1)
                    mm(bank[1][:, 0:2 * C], hTh[:, f, :], w2f[:, bass.ds(at2 + f * 2 * C, 2 * C)], start=f == 0, stop=False)
                    mm(bank[1][:, 0:C], hTl[:, f, :], w2f[:, bass.ds(at2 + f * 2 * C, C)], start=False, stop=False)
                mm(bank[1][:, 0:C], ones2[:, :], b2r[:, bass.ds(e * C, C)], start=False, stop=True).then_inc(p_dn, 1)

            pe.wait_ge(v_tab, 12)
            pe.wait_ge(s_lo, NCH)
            pe.wait_ge(s_rows, 16 * 2 * (E + 1))
            e_now = expert(0)
            rows_in(0, 0, 16)
            up(0, e_now)
            rows_in(1, 1, 16)

            def blk(b, par, nxt, done):
                hidT(b)
                if nxt >= 1:
                    up(b + 1, expert(b + 1))
                if nxt >= 2:
                    rows_in(b + 2, par, done)
                down(b, expert(b))

            blk(0, 0, 2, 32)
            blk(1, 1, 2, 32)
            with pe.Fori(1, (NBLK - 2) // 2) as i:
                blk(2 * i, 0, 2, 16 * i + 32)
                blk(2 * i + 1, 1, 2, 16 * i + 32)
            for b in range((NBLK - 2) // 2 * 2, NBLK):
                blk(b, b % 2, min(2, NBLK - 1 - b), 16 * (b // 2) + 32)

            for t in range(NT):
                pe.wait_ge(v_z, t + 1)
                if t >= 2:
                    pe.wait_ge(a_z, t - 1)
                for k in range(2):
                    ins = pe.transpose(bank[2 + t % 2][0:CH, k * P:(k + 1) * P], z[t % 2][:, k * CH:(k + 1) * CH], ident)
                ins.then_inc(p_z, 1)


_OUT = ((B, C, IMG, IMG), "float32")


def kernel(x, L0_conv_Wq, L0_conv_Wk, L0_conv_Wv, L0_conv_Wo_w, L0_conv_Wo_b, L0_conv_rel_pos_bias,
           L0_conv_rel_coords, L0_ffn_gate_w, L0_ffn_gate_b, L0_ffn_w1, L0_ffn_b1, L0_ffn_w2, L0_ffn_b2):
    import concourse.bacc as _bacc
    from concourse.bass_utils import run_bass_kernel_spmd as _run

    c, table, places = constants()
    arrays = {
        "x": x, "wqT": np.asarray(L0_conv_Wq).T, "wkT": np.asarray(L0_conv_Wk).T, "wvT": np.asarray(L0_conv_Wv).T,
        "woT": np.asarray(L0_conv_Wo_w).T, "wo_b": L0_conv_Wo_b, "relT": np.asarray(L0_conv_rel_pos_bias).T,
        "coords": np.asarray(L0_conv_rel_coords).reshape(-1), "gate_w": L0_ffn_gate_w, "gate_b": L0_ffn_gate_b,
        "w1": L0_ffn_w1, "b1": L0_ffn_b1, "w2": L0_ffn_w2, "b2": L0_ffn_b2, "const_d": c, "table_d": table, "place_d": places,
    }
    arrays = {f"in_{n}": np.ascontiguousarray(a) for n, a in arrays.items()}
    nc = _bacc.Bacc("TRN2", target_bir_lowering=False, num_devices=1)
    args = [nc.dram_tensor(n, a.shape, mybir.dt.from_np(a.dtype), kind="ExternalInput").ap() for n, a in arrays.items()]
    args.append(nc.dram_tensor("out_0", _OUT[0], mybir.dt.from_np(np.dtype(_OUT[1])), kind="ExternalOutput").ap())
    program(nc, *args)
    r = _run(nc, [arrays], core_ids=[0])
    return r.results[0]["out_0"]
```

```python
import concourse.bass as bass
from concourse import mybir
from contextlib import ExitStack
import numpy as np


B, C, IMG = 8, 192, 16
WIN = 8
L = WIN * WIN
NH, HD = 12, 16
P = 128
N = B * IMG * IMG
NT = N // P
CH = C // 2
PAIRS = CH // (2 * HD)
E, F = 6, 768
FT = F // P
NREL = (2 * WIN - 1) ** 2
CAP = N + P
PADROW = E * CAP
NBLK = (2 * N + E * (P - 1)) // P
ROW = C + 2
SKIP = 1 << 20
REST = C - P
NCH = 2 * E
HW_F = F // 2
RC = 512
NSTEP = L * L // RC
NLOAD = 10
TAB_PADS, TAB_BLOCKS = 2, 12

_at = {}
_n = 0
for _name, _w in (("ident", P), ("before", P), ("parity", 2), ("experts", 2 * E), ("region", E),
                  ("relrow", 2)):
    _at[_name] = (_n, _n + _w)
    _n += _w
NCONST = _n


def constants():
    c = np.zeros((P, NCONST), np.float32)
    p = np.arange(P)

    def put(name, v):
        a, b = _at[name]
        c[:, a:b] = v

    put("ident", np.eye(P))
    put("before", p[:, None] < p[None, :])
    put("parity", (p[:, None] // HD) % 2 == np.arange(2)[None, :])
    put("experts", np.tile(np.arange(E), 2)[None, :])
    put("region", (np.arange(E) * CAP)[None, :])
    put("relrow", p[:, None] + P * np.arange(2)[None, :])
    table = np.concatenate([np.repeat(np.arange(NBLK), E), (np.arange(E)[None, :] <= np.arange(E)[:, None]).reshape(-1),
                            np.arange(NBLK) * P]).astype(np.float32)[None, :]
    place = 2 * (p[:, None, None] + P * np.arange(NT)[None, :, None]) + np.arange(2)[None, None, :]
    places = np.concatenate([place.reshape(P, 2 * NT), np.full((P, 1), SKIP)], 1).astype(np.int32)
    return c, table, places


def program(nc, x, wqT, wkT, wvT, woT, wo_b, relT, coords, gate_w, gate_b, w1, b1, w2, b2,
            const_d, table_d, place_d, out):
    f32, f32r, i32, u32 = mybir.dt.float32, mybir.dt.float32r, mybir.dt.int32, mybir.dt.uint32
    bf16 = mybir.dt.bfloat16
    ALU, ACT, AX = mybir.AluOpType, mybir.ActivationFunctionType, mybir.AxisListType
    NEG = -3.0e38

    bias_d = nc.dram_tensor("bias_d", [NH, L * L], f32, kind="Internal").ap()
    routed = nc.dram_tensor("routed", [PADROW + P, ROW], f32, kind="Internal").ap()
    made = nc.dram_tensor("made", [2 * N, C], f32, kind="Internal").ap()

    with ExitStack() as ctx:
        def sb(name, shape, dt=f32):
            return ctx.enter_context(nc.sbuf_tensor(name, shape, dt))

        def sem(name):
            return ctx.enter_context(nc.semaphore(name))

        cst = sb("cst", [P, NCONST])
        places = sb("places", [P, 2 * NT + 1], i32)
        wq, wk, wv = (sb(n, [CH, 2, C]) for n in ("wq", "wk", "wv"))
        wo = sb("wo", [CH + 1, 2, C])
        gw = sb("gw", [CH + 1, 2, E])
        w1h, w1m, w1l = (sb(n, [P, E, F], f32r) for n in ("w1h", "w1m", "w1l"))
        w1e = sb("w1e", [REST + 2, E, F], f32r)
        w2s = sb("w2s", [P, E * FT, 2 * C], f32r)
        b2r = sb("b2r", [2, E * C], f32r)
        raw1 = [sb(f"raw1_{n}", [P, F]) for n in range(2)]
        raw2 = [sb(f"raw2_{n}", [P, FT // 2, C]) for n in range(2)]
        bias = sb("bias", [P, NH, L])
        ones = sb("ones", [P, P], bf16)
        earlier = sb("earlier", [P, P], bf16)
        ones2 = sb("ones2", [2, P], f32r)
        arena = sb("arena", [P, 4 * RC])
        crd = [arena[:, n * RC:(n + 1) * RC].bitcast(i32) for n in range(2)]
        bT = [arena[0:NH, (2 + n) * RC:(3 + n) * RC] for n in range(2)]
        c_block = arena[0:1, 3 * RC:3 * RC + NBLK * E].rearrange("p (a b) -> p a b", a=NBLK)
        c_upto = arena[0:1, 3 * RC + NBLK * E:3 * RC + NBLK * E + E * E].rearrange("p (a b) -> p a b", a=E)
        c_row = arena[0:1, 3 * RC + (NBLK + E) * E:3 * RC + (NBLK + E) * E + NBLK]
        c_all = arena[0:1, 3 * RC:3 * RC + (NBLK + E) * E + NBLK]
        split = sb("split", [P, 4 * RC], f32r)
        hot = [split[:, n * 2 * RC:(n + 1) * 2 * RC].rearrange("p (k c) -> p k c", k=2) for n in range(2)]
        hTh = split[:, 0:F].rearrange("p (f t) -> p f t", f=FT)
        hTl = split[:, F:2 * F].rearrange("p (f t) -> p f t", f=FT)
        relraw = sb("relraw", [P, 2, NH])
        relh = sb("relh", [P, 2, NH], f32r)
        rell = sb("rell", [P, 2, NH], f32r)
        ytok = sb("ytok", [P, NT, C])
        b1raw, b2raw = raw1[1][0:E, :], raw2[1][0:E, 0, :]
        b1parts = [w1l[0:E, E - 1 - k, :] for k in range(2)]
        b2parts = [w1l[0:E, E - 3, k * C:(k + 1) * C] for k in range(2)]
        xin = sb("xin", [CH, 2, P])
        xpad = sb("xpad", [P, ROW])
        xn = xpad[:, 0:C]
        xnT = sb("xnT", [CH, 2, P])
        qT = sb("qT", [CH, 2, P])
        kbd = sb("kbd", [CH, 2, 2, 2, L])
        vbd = [sb(f"vbd{n}", [P, 2, NH // 2, 2, HD + 1]) for n in range(2)]
        prob = [sb(f"prob{n}", [P, NH, L]) for n in range(2)]
        pT = sb("pT", [P, NH // 2, P])
        hid = pT[:, :, :].rearrange("p a b -> p (a b)")
        oT = sb("oT", [CH + 1, 2, P])
        rmax = sb("rmax", [P, NH])
        inv = sb("inv", [P, NH])
        osb = sb("osb", [P, C])
        st, st2 = sb("st", [P, 6]), sb("st2", [P, 6])
        mv, mv2 = sb("mv", [P, 2]), sb("mv2", [P, 2])
        veps, veps2, rstd, rstd2, half_neg = (sb(n, [P, 1]) for n in ("veps", "veps2", "rstd", "rstd2", "half_neg"))
        row = [[sb(f"row{n}{k}", [P, ROW]) for k in range(2)] for n in range(2)]
        rowin = [row[n][0] for n in range(2)]
        yrow = [row[n][1] for n in range(2)]
        xlT = sb("xlT", [CH + 1, 2, P])
        score = sb("score", [P, 8])
        top = sb("top", [P, 8])
        topi = sb("topi", [P, 8], u32)
        topf = sb("topf", [P, 2])
        pick = [sb(f"pick{n}", [P, 2, E]) for n in range(2)]
        cnt = [sb(f"cnt{n}", [P, E], bf16) for n in range(2)]
        seen = sb("seen", [P, E], bf16)
        slot_e = sb("slot_e", [P, E])
        slot_p = sb("slot_p", [P, 2, E])
        slot_f = sb("slot_f", [P, 2])
        slot = [sb(f"slot{n}", [P, 2], i32) for n in range(2)]
        tops = sb("tops", [P, NT, 2])
        gates = sb("gates", [P, 2, NT])
        gtmp = sb("gtmp", [P, NT])
        tot_i, nb_i, pad_i = (sb(n, [1, E], i32) for n in ("tot_i", "nb_i", "pad_i"))
        tot_f, nb_f, last_f, pad_f = (sb(n, [1, E]) for n in ("tot_f", "nb_f", "last_f", "pad_f"))
        tri = arena[0:1, 0:E * E].rearrange("p (a b) -> p a b", a=E)
        past, past_n = (arena[0:1, n * RC:n * RC + NBLK * E].rearrange("p (a b) -> p a b", a=NBLK) for n in (1, 2))
        exp_f, base_f, off_f = (sb(n, [1, NBLK]) for n in ("exp_f", "base_f", "off_f"))
        exp_i, off_i = (sb(n, [1, NBLK], i32) for n in ("exp_i", "off_i"))
        xh, xl, xm, xe = (split[:, 2 * F + n * P:2 * F + (n + 1) * P] for n in range(4))
        ylow = prob[0][:, 6:9, :].rearrange("p a b -> p (a b)")
        ring = sb("ring", [P, NBLK], i32)
        dest = [sb(f"dest{n}", [P, 1], i32) for n in range(2)]
        free = [arena[:, n * 4 * P:(n + 1) * 4 * P] for n in range(4)]
        free += [bias[:, :, :].rearrange("p a b -> p (a b)"), hid, raw1[0], raw1[1]]
        oc = [part[0:CH, 0:4 * P].rearrange("p (k n) -> p k n", k=2) for part in free]
        back = w2s[:, 0:NT, :].bitcast(f32)
        z = [prob[n % 2][:, n // 2 * 3:n // 2 * 3 + 3, :].rearrange("p a b -> p (a b)") for n in range(4)]

        bank = [ctx.enter_context(nc.psum_tensor(f"bank{n}", [P, 512], f32)) for n in range(4)]
        up_ps = ctx.enter_context(nc.psum_tensor("up_ps", [P, 4, 512], f32))
        s_ps = up_ps[:, 0:3, 0:2 * P]
        bank7 = up_ps[:, 3, :]

        def banks_pT(t):
            a, b = (up_ps[:, 0, :], up_ps[:, 1, :]) if t.last() else (bank7, bank[3])
            return a[:, 0:3 * P], b[:, 0:3 * P]

        def bank_o(t):
            return up_ps[:, 2, :] if t.last() else bank[1]

        ident = cst[:, slice(*_at["ident"])]
        before = cst[:, slice(*_at["before"])]
        parity = cst[:, slice(*_at["parity"])]
        experts = cst[:, slice(*_at["experts"])].rearrange("p (k e) -> p k e", k=2)
        region = cst[:, slice(*_at["region"])]
        relrow = cst[:, slice(*_at["relrow"])]

        s_const, s_bload = sem("s_const"), sem("s_bload")
        s_crd = [sem("s_crd0"), sem("s_crd1")]
        s_xin = sem("s_xin")
        s_raw = [sem("s_raw0"), sem("s_raw1")]
        s_set, s_rel, s_apart = sem("s_set"), sem("s_rel"), sem("s_apart")
        s_parts, s_rows = sem("s_parts"), sem("s_rows")
        s_hot, s_bmm, s_bev, s_bias = (sem(n) for n in ("s_hot", "s_bmm", "s_bev", "s_bias"))
        s_bout = [sem("s_bout0"), sem("s_bout1")]
        s_hi, s_lo = sem("s_hi"), sem("s_lo")
        (p_x, p_xn, p_qk, p_v, p_s, p_pT, p_o, p_oT, p_y, p_xl, p_gate, p_pos) = (
            sem(n) for n in ("p_x", "p_xn", "p_qk", "p_v", "p_s", "p_pT", "p_o", "p_oT", "p_y", "p_xl", "p_gate", "p_pos"))
        a_qk, a_exp, a_pT, a_xn, a_xl, a_row, a_o, a_v = (
            sem(n) for n in ("a_qk", "a_exp", "a_pT", "a_xn", "a_xl", "a_row", "a_o", "a_v"))
        v_max, v_sub, v_x, v_mv, v_xn, v_inv, v_o = (
            sem(n) for n in ("v_max", "v_sub", "v_x", "v_mv", "v_xn", "v_inv", "v_o"))
        v_sc, v_top, v_topi, v_topf, v_pick, v_cnt = (
            sem(n) for n in ("v_sc", "v_top", "v_topi", "v_topf", "v_pick", "v_cnt"))
        v_y, v_st2, v_mv2, v_xl, v_pos, v_sp, v_sf, v_slot, v_seen = (
            sem(n) for n in ("v_y", "v_st2", "v_mv2", "v_xl", "v_pos", "v_sp", "v_sf", "v_slot", "v_seen"))
        g_ve, g_rs, g_ve2, g_rs2, g_dst = (sem(n) for n in ("g_ve", "g_rs", "g_ve2", "g_rs2", "g_dst"))
        s_scat = [sem("s_scat0"), sem("s_scat1")]
        p_tot, v_tab, v_gate, a_gate, s_pad = (sem(n) for n in ("p_tot", "v_tab", "v_gate", "a_gate", "s_pad"))
        s_rowin = [sem("s_rowin0"), sem("s_rowin1")]
        p_bx, p_up, p_hT, p_dn = (sem(n) for n in ("p_bx", "p_up", "p_hT", "p_dn"))
        a_hi, a_gelu, a_ylow = (sem(n) for n in ("a_hi", "a_gelu", "a_ylow"))
        v_lo, v_bxh, v_bx, v_ring, v_yrow = (sem(n) for n in ("v_lo", "v_bxh", "v_bx", "v_ring", "v_yrow"))
        s_made = [sem("s_made0"), sem("s_made1")]
        s_back = [sem(f"s_back{n}") for n in range(B)]
        s_table = sem("s_table")
        v_z1, v_z, p_z, a_z = (sem(n) for n in ("v_z1", "v_z", "p_z", "a_z"))
        s_out = sem("s_out")

        FIRST, LAST = -2, NT + 2
        LOOP_A, LOOP_B = 2, NT // 2 - 1

        class Tile:

            def __init__(self, i, d):
                self.n, self.par, self.fixed = 2 * i + d, d % 2, isinstance(i, int)
                self.pair = i + d // 2

            def there(self, ahead=0):
                return not self.fixed or 0 <= self.n + ahead < NT

            def last(self):
                return self.fixed and self.n == NT - 1

            def after(self, k):
                return not self.fixed or self.n >= k

        def wait_apart(eng, semaphore, value):
            eng.wait_ge(semaphore, value)
            eng.sem_inc(s_apart, 1)

        def windows(ap):
            return ap.rearrange("p (i w j) -> p w i j", i=WIN, w=2)

        def windowed(ap):
            return ap.rearrange("p (w i j) -> p w i j", w=2, i=WIN)

        w2_v = w2.rearrange("e (k f p) n -> (e k) p f n", k=2, p=P)
        x_v = x.rearrange("b (k p) h w -> b p k (h w)", p=CH)
        out_v = out.rearrange("b (k p) h w -> b p k (h w)", p=CH)
        made_v = made.rearrange("(b t p k) c -> b p t (k c)", b=B, p=P, k=2)

        block = ctx.enter_context(nc.Block())

        def pad_rows(eng, first):
            eng.wait_ge(g_dst, 3)
            eng.wait_ge(v_tab, TAB_PADS)
            for e in range(first, E, 2):
                at = eng.value_load(pad_i[0:1, e:e + 1], min_val=e * CAP, max_val=e * CAP + N)
                eng.dma_start(routed[bass.ds(at, P), :], xpad[:, :]).then_inc(s_pad, 16)

        @block.sync
        def _(sp):
            def load_x(t):
                if not t.there():
                    return
                if t.after(1):
                    sp.wait_ge(p_x, t.n)
                sp.dma_start(xin[:, :, :], x_v[bass.ds(t.pair, 1), :, :, t.par * P:(t.par + 1) * P]
                             .rearrange("b p k n -> (b p) k n")).then_inc(s_xin, 16)

            def load_chunk(i, r):
                c = 2 * i + r
                if isinstance(i, int) and not 0 <= c < NCH:
                    return
                if not isinstance(i, int) or c >= 2:
                    sp.wait_ge(s_lo, c - 1)
                if r == 0:
                    sp.dma_start(raw1[0][:, :], w1[bass.ds(i, 1), 0:P, :].rearrange("a p f -> (a p) f")).then_inc(s_raw[0], 16)
                else:
                    for n in range(2):
                        sp.dma_start(raw1[1][n * REST:(n + 1) * REST, :],
                                     w1[bass.ds(i, 1), P:C, :].rearrange("a p f -> (a p) f")).then_inc(s_raw[1], 16)
                sp.dma_start(raw2[r][:, :, :], w2_v[bass.ds(c, 1), :, :, :].rearrange("a p f n -> (a p) f n")).then_inc(s_raw[r], 16)

            def load_bias(half):
                for n in range(2):
                    sp.wait_ge(s_bout[n], 16 * (NSTEP // 4) * (half + 1))
                a, b = half * L // 2, (half + 1) * L // 2
                for w in range(2):
                    sp.dma_start(bias[w * L + a:w * L + b, :, :],
                                 bias_d.rearrange("h (l m) -> l h m", l=L)[a:b, :, :]).then_inc(s_bias, 16)

            load_x(Tile(0, 0))
            for n in range(2):
                sp.dma_start(crd[n], coords[n * RC:(n + 1) * RC].partition_broadcast(P)).then_inc(s_crd[n], 16)
            for n in range(2, NSTEP):
                sp.wait_ge(s_hot, n - 1)
                sp.dma_start(crd[n % 2], coords[n * RC:(n + 1) * RC].partition_broadcast(P)).then_inc(s_crd[n % 2], 16)
                if n == NSTEP // 2 + 1:
                    load_x(Tile(0, 1))
            load_bias(0)
            load_bias(1)

            def slot_(i, r):
                load_x(Tile(i, r + 3))
                load_chunk(i, r)

            slot_(-1, 1)
            sp.wait_ge(s_parts, 2)
            for k in range(2):
                sp.dma_start(w1e[REST + k:REST + k + 1, :, :].bitcast(f32),
                             b1parts[k].bitcast(f32)).then_inc(s_rows, 16)
                sp.dma_start(b2r[k:k + 1, :].bitcast(f32), b2parts[k].bitcast(f32)).then_inc(s_rows, 16)
            for s in range(0, 2 * LOOP_A):
                slot_(s // 2, s % 2)
            with sp.Fori(LOOP_A, NCH // 2) as i:
                slot_(i, 0)
                slot_(i, 1)
            for s in range(NCH, LAST):
                slot_(s // 2, s % 2)
            sp.wait_ge(s_hot, NSTEP)
            sp.dma_start(c_all, table_d).then_inc(s_table, 16)

            pad_rows(sp, 0)
            sp.dma_start(routed[PADROW:PADROW + P, :], xpad[:, :]).then_inc(s_pad, 16)
            for n in range(2):
                sp.wait_ge(s_scat[n], 32 * (NT // 2))
            sp.wait_ge(s_pad, 16 * (E + 1))
            sp.wait_ge(v_tab, TAB_BLOCKS)

            def load_rows(b, par):
                if not isinstance(b, int) or b >= 2:
                    sp.wait_ge(v_ring, b - 1)
                at = sp.value_load(off_i[0:1, bass.ds(b, 1)], min_val=0, max_val=PADROW)
                sp.dma_start(rowin[par][:, :], routed[bass.ds(at, P), :]).then_inc(s_rowin[par], 16)

            load_rows(0, 0)
            load_rows(1, 1)
            with sp.Fori(1, NBLK // 2) as i:
                load_rows(2 * i, 0)
                load_rows(2 * i + 1, 1)
            if NBLK % 2:
                load_rows(NBLK - 1, 0)

            for n in range(2):
                sp.wait_ge(s_made[n], 16 * ((NBLK + 1 - n) // 2))
            for b in range(B):
                sp.dma_start(back[:, 2 * b:2 * b + 2, :], made_v[b]).then_inc(s_back[b], 16)
            for b in range(B):
                sp.wait_ge(a_z, b + 1)
                sp.dma_start(out_v[b], oc[b]).then_inc(s_out, 16)
            sp.wait_ge(s_out, 16 * B)

        @block.gpsimd
        def _(pool):
            def rstd_of(t, ready, mv_, veps_, rstd_, g_v, g_r, eps):
                if not t.there():
                    return
                wait_apart(pool, ready, t.n + 1)
                pool.tensor_scalar(veps_[:, :], mv_[:, 1:2], eps, None, ALU.add).then_inc(g_v, 1)
                pool.wait_ge(g_v, t.n + 1)
                pool.tensor_tensor(rstd_[:, :], veps_[:, :], half_neg[:, :], ALU.pow).then_inc(g_r, 1)

            def slot_(i, r):
                rstd_of(Tile(i, r - 2), v_mv2, mv2, veps2, rstd2, g_ve2, g_rs2, 1e-5)
                rstd_of(Tile(i, r + 2), v_mv, mv, veps, rstd, g_ve, g_rs, 1e-6)
                c = 2 * i + r - 1
                if not isinstance(i, int) or 0 <= c < NCH:
                    pool.wait_ge(s_hi, c + 1)
                    n = (P, REST)[1 - r]
                    pool.tensor_tensor((w1l, w1e)[1 - r][0:n, bass.ds(i - 1 + r, 1), :].rearrange("p a f -> p (a f)"),
                                       raw1[1 - r][0:n, :],
                                       (w1h, w1m)[1 - r][0:n, bass.ds(i - 1 + r, 1), :].rearrange("p a f -> p (a f)")
                                       .bitcast(f32), ALU.subtract)
                    pool.tensor_tensor(w2s[:, bass.ds(c * (FT // 2), FT // 2), C:2 * C], raw2[1 - r][:, :, :],
                                       w2s[:, bass.ds(c * (FT // 2), FT // 2), 0:C].bitcast(f32),
                                       ALU.subtract).then_inc(s_lo, 1)
                t = Tile(i, r - 3)
                if t.there():
                    pool.wait_ge(a_row, t.n + 1)
                    wait_apart(pool, v_slot, t.n + 1)
                    for k in range(2):
                        pool.indirect_dma_start(
                            out=routed[:, :], out_offset=bass.IndirectOffsetOnAxis(ap=slot[t.par][:, k:k + 1], axis=0),
                            in_=row[t.par][k][:, :], in_offset=None).then_inc(s_scat[t.par], 16)

            pool.wait_ge(s_set, 1)
            for s in range(FIRST, 2 * LOOP_A):
                slot_(s // 2, s % 2)
            pool.wait_ge(s_rows, 16 * 4)
            with pool.Fori(LOOP_A, NCH // 2) as i:
                slot_(i, 0)
                slot_(i, 1)
            for s in range(NCH, NT):
                slot_(s // 2, s % 2)
            pool.wait_ge(p_xn, NT)
            pool.memset(xpad[:, :], 0.0).then_inc(g_dst, 1)
            pool.wait_ge(g_dst, 1)
            pool.tensor_copy(xpad[:, C:C + 1].bitcast(i32), places[:, 2 * NT:2 * NT + 1]).then_inc(g_dst, 2)
            for s in range(NT, LAST + 1):
                slot_(s // 2, s % 2)

            bound = pool.to_reg(2 * N - 1)

            def store_rows(b, par):
                wait_apart(pool, v_yrow, b + 1)
                pool.indirect_dma_start(
                    out=made[:, :], out_offset=bass.IndirectOffsetOnAxis(ap=dest[par][:, :], axis=0),
                    in_=yrow[par][:, 0:C], in_offset=None, bounds_check=bound, oob_is_err=False).then_inc(s_made[par], 16)

            with pool.Fori(0, NBLK // 2) as i:
                store_rows(2 * i, 0)
                store_rows(2 * i + 1, 1)
            if NBLK % 2:
                store_rows(NBLK - 1, 0)

        @block.scalar
        def _(act):
            act.dma_start(relraw[:, 0, :], relT[0:P, :]).then_inc(s_const, 16)
            act.dma_start(relraw[0:NREL - P, 1, :], relT[P:NREL, :]).then_inc(s_const, 16)
            act.dma_start(cst[:, :], const_d).then_inc(s_const, 16)
            act.dma_start(places[:, :], place_d).then_inc(s_bload, 16)
            for w_sb, w_dr in ((wq, wqT), (wk, wkT), (wv, wvT), (wo, woT), (gw, gate_w)):
                act.dma_start(w_sb[0:CH, :, :], w_dr.rearrange("(k p) n -> p k n", p=CH)).then_inc(s_bload, 16)
            act.dma_start(wo[CH:CH + 1, 1, :], wo_b.unsqueeze(0)).then_inc(s_bload, 16)
            act.dma_start(gw[CH:CH + 1, 1, :], gate_b.unsqueeze(0)).then_inc(s_bload, 16)
            act.dma_start(b1raw, b1).then_inc(s_bload, 16)
            act.dma_start(b2raw, b2).then_inc(s_bload, 16)

            def bias_out(n):
                act.wait_ge(s_bmm, n + 1)
                if n >= 2:
                    act.wait_ge(s_bout[n % 2], 16 * (n // 2))
                act.activation(bT[n % 2], bank[2 + n % 2][0:NH, :], ACT.Copy).then_inc(s_bev, 1)
                act.wait_ge(s_bev, n + 1)
                act.dma_start(bias_d[:, n * RC:(n + 1) * RC], bT[n % 2]).then_inc(s_bout[n % 2], 16)

            for n in range(NSTEP // 2):
                bias_out(n)

            def slot_(i, r):
                t = Tile(i, r - 1)
                if t.there():
                    act.wait_ge(p_pT, t.n + 1)
                    if t.after(1):
                        act.wait_ge(p_o, t.n)
                    act.activation(pT[:, 0:3, :], banks_pT(t)[0].rearrange("p (a b) -> p a b", a=3), ACT.Copy)
                    act.activation(pT[:, 3:6, :], banks_pT(t)[1].rearrange("p (a b) -> p a b", a=3), ACT.Copy).then_inc(a_pT, 1)
                t = Tile(i, r - 2)
                if t.there():
                    act.wait_ge(p_xl, t.n + 1)
                    if t.after(1):
                        act.wait_ge(p_gate, t.n)
                    act.activation(xlT[0:CH, :, :], bank7[0:CH, 0:2 * P].rearrange("p (k n) -> p k n", k=2),
                                   ACT.Copy).then_inc(a_xl, 1)
                t = Tile(i, r)
                if t.there():
                    act.wait_ge(v_sub, t.n + 1)
                    p3 = prob[t.par][:, :, :]
                    act.activation(p3, p3, ACT.Exp).then_inc(a_exp, 1)
                t = Tile(i, r + 1)
                if t.there():
                    act.wait_ge(p_qk, t.n + 1)
                    if t.after(1):
                        act.wait_ge(p_s, t.n)
                    act.activation(qT[:, :, :], bank[2][0:CH, 0:2 * P].rearrange("p (k n) -> p k n", k=2),
                                   ACT.Copy, scale=float(HD) ** -0.5)
                    for h in range(2):
                        ins = act.activation(kbd[:, :, :, h, :],
                                             bank[2][0:CH, 2 * P:4 * P].rearrange("p (k w m) -> p k w m", k=2, w=2),
                                             ACT.Copy, scale=parity[0:CH, h:h + 1])
                    ins.then_inc(a_qk, 1)
                t = Tile(i, r - 1)
                if t.there():
                    act.wait_ge(p_oT, t.n + 1)
                    if t.after(1):
                        act.wait_ge(p_y, t.n)
                    for k in range(2):
                        ins = act.activation(windows(oT[0:CH, k, :]), windowed(bank_o(t)[0:CH, k * P:(k + 1) * P]), ACT.Copy)
                    ins.then_inc(a_o, 1)
                t = Tile(i, r + 2)
                if t.there():
                    act.wait_ge(p_xn, t.n + 1)
                    if t.after(1):
                        act.wait_ge(p_v, t.n)
                    for k in range(2):
                        ins = act.activation(windowed(xnT[:, k, :]), windows(bank[0][0:CH, k * P:(k + 1) * P]), ACT.Copy)
                    ins.then_inc(a_xn, 1)
                t = Tile(i, r - 2)
                if t.there():
                    if t.after(2):
                        act.wait_ge(s_scat[t.par], 32 * t.pair)
                    act.activation(row[t.par][1][:, 0:C], row[t.par][0][:, 0:C], ACT.Copy).then_inc(a_row, 1)
                t = Tile(i, r + 1)
                if t.there():
                    act.wait_ge(p_v, t.n + 1)
                    if t.after(2):
                        act.wait_ge(p_o, t.n - 1)
                    for h in range(2):
                        for w in range(2):
                            ins = act.activation(
                                vbd[t.par][h * L:(h + 1) * L, w, :, h, 0:HD],
                                bank[3][w * L:(w + 1) * L, 0:C].rearrange("p (j h d) -> p j h d", h=2, d=HD)[:, :, h, :], ACT.Copy)
                    ins.then_inc(a_v, 1)
                c = 2 * i + r
                if not isinstance(i, int) or 0 <= c < NCH:
                    act.wait_ge(s_raw[r], (32 + 16 * r) * (i + 1))
                    act.activation((w1h, w1m)[r][:, bass.ds(i, 1), :].rearrange("p a f -> p (a f)"), raw1[r][:, :], ACT.Copy)
                    act.activation(w2s[:, bass.ds(c * (FT // 2), FT // 2), 0:C], raw2[r][:, :, :],
                                   ACT.Copy).then_inc(s_hi, 1)

            slot_(-1, 0)
            for n in range(NSTEP // 2, NSTEP):
                bias_out(n)
            for s in range(FIRST + 1, 2 * LOOP_A):
                slot_(s // 2, s % 2)
            with act.Fori(LOOP_A, NCH // 2) as i:
                slot_(i, 0)
                slot_(i, 1)
            for s in range(NCH, LAST):
                slot_(s // 2, s % 2)
            pad_rows(act, 1)
            act.wait_ge(v_gate, 1)
            act.activation(gates[:, 1, :], gtmp[:, :], ACT.Exp).then_inc(a_gate, 1)

            def gelu(b):
                act.wait_ge(p_up, b + 1)
                if not isinstance(b, int) or b >= 1:
                    act.wait_ge(p_hT, b)
                act.activation(hid.rearrange("p (n c) -> p n c", n=2), up_ps[:, 0:2, 0:HW_F], ACT.Gelu).then_inc(a_gelu, 1)

            def hi(b):
                act.wait_ge(p_hT, b + 1)
                if not isinstance(b, int) or b >= 1:
                    act.wait_ge(p_dn, b)
                for n in range(2):
                    act.activation(hTh[:, 3 * n:3 * n + 3, :], up_ps[:, 2 + n, 0:3 * P].rearrange("p (a b) -> p a b", a=3),
                                   ACT.Copy).then_inc(a_hi, 1)

            def ylow_(b):
                act.wait_ge(p_dn, b + 1)
                if not isinstance(b, int) or b >= 1:
                    act.wait_ge(v_yrow, b)
                act.activation(ylow[:, :], bank[1][:, C:2 * C], ACT.Copy).then_inc(a_ylow, 1)

            gelu(0)
            hi(0)
            gelu(1)
            ylow_(0)
            with act.Fori(1, NBLK - 1) as b:
                hi(b)
                gelu(b + 1)
                ylow_(b)
            hi(NBLK - 1)
            ylow_(NBLK - 1)

            for b in range(B):
                act.wait_ge(p_z, 2 * b + 2)
                act.activation(oc[b], bank[2 + b % 2][0:CH, :].rearrange("p (k n) -> p k n", k=2),
                               ACT.Copy).then_inc(a_z, 1)

        @block.vector
        def _(dve):
            dve.memset(ones[:, :], 1.0)
            dve.memset(ones2[:, :].bitcast(f32), 1.0)
            dve.memset(oT[CH:CH + 1, :, :], 1.0)
            dve.memset(xlT[CH:CH + 1, :, :], 1.0)
            dve.memset(half_neg[:, :], -0.5)
            for n in range(2):
                dve.memset(vbd[n][:, :, :, :, :], 0.0)
                for k in range(2):
                    dve.memset(row[n][k][:, C:ROW], 0.0)
            dve.memset(score[:, :], NEG)
            dve.memset(seen[:, :], 0.0).then_inc(s_set, 1)
            dve.wait_ge(s_set, 1)
            for n in range(2):
                for h in range(2):
                    ins = dve.memset(vbd[n][h * L:(h + 1) * L, :, :, h, HD], 1.0)
            ins.then_inc(s_set, 1)
            dve.wait_ge(s_const, 16 * 3)
            dve.tensor_copy(earlier[:, :], before)
            dve.tensor_copy(relh[:, 0, :], relraw[:, 0, :])
            dve.tensor_copy(relh[0:NREL - P, 1, :], relraw[0:NREL - P, 1, :]).then_inc(s_rel, 1)
            dve.wait_ge(s_rel, 1)
            dve.tensor_tensor(rell[:, 0, :], relraw[:, 0, :], relh[:, 0, :].bitcast(f32), ALU.subtract)
            dve.tensor_tensor(rell[0:NREL - P, 1, :], relraw[0:NREL - P, 1, :],
                              relh[0:NREL - P, 1, :].bitcast(f32), ALU.subtract).then_inc(s_rel, 1)

            def one_hots(n):
                dve.wait_ge(s_crd[n % 2], 16 * (n // 2 + 1))
                if n >= 2:
                    dve.wait_ge(s_bmm, n - 1)
                for k in range(2):
                    ins = dve.tensor_scalar(hot[n % 2][:, k, :], crd[n % 2], relrow[:, k:k + 1], None, ALU.is_equal)
                ins.then_inc(s_hot, 1)

            def slot_(i, r):
                t = Tile(i, r + 2)
                if t.there():
                    dve.wait_ge(p_x, t.n + 1)
                    dve.tensor_copy(ytok[:, bass.ds(t.n, 1), :].rearrange("p a c -> p (a c)"), bank[0][:, 0:C])
                    if t.after(1):
                        wait_apart(dve, v_mv, t.n)
                    dve.bn_stats(st[:, :], bank[0][:, 0:C]).then_inc(v_x, 1)
                    if t.after(1):
                        dve.wait_ge(g_ve, t.n)
                        dve.wait_ge(v_xn, t.n)
                    wait_apart(dve, v_x, t.n + 1)
                    dve.bn_aggr(mv[:, :], st[:, :]).then_inc(v_mv, 1)
                t = Tile(i, r - 2)
                if t.there():
                    dve.wait_ge(g_rs2, t.n + 1)
                    if t.after(2):
                        dve.wait_ge(s_scat[t.par], 32 * t.pair)
                    dve.tensor_scalar(row[t.par][0][:, 0:C], ytok[:, bass.ds(t.n, 1), :].rearrange("p a c -> p (a c)"),
                                      mv2[:, 0:1], rstd2[:, 0:1], ALU.subtract, ALU.mult).then_inc(v_xl, 1)
                t = Tile(i, r)
                if t.there():
                    dve.wait_ge(p_s, t.n + 1)
                    if t.after(1):
                        dve.wait_ge(v_sub, t.n)
                    for k in range(2):
                        ins = dve.tensor_reduce(rmax[:, 6 * k:6 * k + 6].rearrange("p (j h) -> p j h", j=PAIRS),
                                                s_ps[:, :, k * P:(k + 1) * P].rearrange("p j (h m) -> p j h m", h=2),
                                                AX.X, ALU.max)
                    ins.then_inc(v_max, 1)
                    dve.wait_ge(v_max, t.n + 1)
                    if t.after(2):
                        dve.wait_ge(p_pT, t.n - 1)
                    for k in range(2):
                        for h in range(2):
                            ins = dve.tensor_tensor(
                                prob[t.par][:, 6 * k:6 * k + 6, :].rearrange("p (j h) m -> p j h m", j=PAIRS)[:, :, h, :],
                                s_ps[:, :, k * P + h * L:k * P + (h + 1) * L],
                                rmax[:, 6 * k:6 * k + 6].rearrange("p (j h) -> p j h", j=PAIRS)[:, :, h]
                                .unsqueeze(2).to_broadcast([P, PAIRS, L]), ALU.subtract)
                    ins.then_inc(v_sub, 1)
                t = Tile(i, r - 1)
                if t.there():
                    dve.wait_ge(p_o, t.n + 1)
                    if t.after(1):
                        dve.wait_ge(v_o, t.n)
                    o3 = bank_o(t)[:, 0:NH * (HD + 1)].rearrange("p (h d) -> p h d", h=NH)
                    dve.reciprocal(inv[:, :], o3[:, :, HD]).then_inc(v_inv, 1)
                    dve.wait_ge(v_inv, t.n + 1)
                    if t.after(1):
                        dve.wait_ge(p_oT, t.n)
                    dve.tensor_tensor(osb[:, :].rearrange("p (h d) -> p h d", h=NH), o3[:, :, 0:HD],
                                      inv[:, :].unsqueeze(2).to_broadcast([P, NH, HD]), ALU.mult).then_inc(v_o, 1)
                t = Tile(i, r + 2)
                if t.there():
                    dve.wait_ge(g_rs, t.n + 1)
                    if t.after(1):
                        dve.wait_ge(p_xn, t.n)
                    dve.tensor_scalar(xn[:, :], ytok[:, bass.ds(t.n, 1), :].rearrange("p a c -> p (a c)"),
                                      mv[:, 0:1], rstd[:, 0:1], ALU.subtract, ALU.mult).then_inc(v_xn, 1)
                t = Tile(i, r - 3)
                if t.there():
                    dve.wait_ge(v_pos, t.n + 1)
                    if t.after(1):
                        dve.wait_ge(v_sf, t.n)
                    dve.tensor_tensor(slot_p[:, :, :], pick[t.par][:, :, :],
                                      slot_e[:, :].unsqueeze(1).to_broadcast([P, 2, E]), ALU.mult).then_inc(v_sp, 1)
                    for k in range(2):
                        dve.tensor_copy(row[t.par][k][:, C:C + 1].bitcast(i32), places[:, bass.ds(2 * t.n + k, 1)])
                    dve.wait_ge(v_sp, t.n + 1)
                    dve.tensor_reduce(slot_f[:, :], slot_p[:, :, :], AX.X, ALU.add).then_inc(v_sf, 1)
                    dve.wait_ge(v_sf, t.n + 1)
                    if t.after(2):
                        dve.wait_ge(s_scat[t.par], 32 * t.pair)
                    dve.tensor_copy(slot[t.par][:, :], slot_f[:, :]).then_inc(v_slot, 1)
                t = Tile(i, r - 2)
                if t.there():
                    dve.wait_ge(p_gate, t.n + 1)
                    if t.after(1):
                        dve.wait_ge(v_topi, t.n)
                    dve.tensor_copy(score[:, 0:E], bank7[:, 0:E]).then_inc(v_sc, 1)
                    wait_apart(dve, v_sc, t.n + 1)
                    dve.max(top[:, :], score[:, :]).then_inc(v_top, 1)
                    wait_apart(dve, v_top, t.n + 1)
                    dve.max_index(topi[:, :], top[:, :], score[:, :]).then_inc(v_topi, 1)
                    dve.tensor_copy(tops[:, bass.ds(t.n, 1), :].rearrange("p a k -> p (a k)"), top[:, 0:2])
                    dve.wait_ge(v_topi, t.n + 1)
                    dve.tensor_copy(topf[:, :], topi[:, 0:2]).then_inc(v_topf, 1)
                    dve.wait_ge(v_topf, t.n + 1)
                    dve.tensor_tensor(pick[t.par][:, :, :], experts, topf[:, :].unsqueeze(2).to_broadcast([P, 2, E]),
                                      ALU.is_equal).then_inc(v_pick, 1)
                    dve.wait_ge(v_pick, t.n + 1)
                    if t.after(2):
                        dve.wait_ge(v_seen, t.n - 1)
                        dve.wait_ge(p_pos, t.n - 1)
                    dve.tensor_tensor(cnt[t.par][:, :], pick[t.par][:, 0, :], pick[t.par][:, 1, :],
                                      ALU.add).then_inc(v_cnt, 1)
                t = Tile(i, r - 1)
                if t.there():
                    dve.wait_ge(p_y, t.n + 1)
                    yt = ytok[:, bass.ds(t.n, 1), :].rearrange("p a c -> p (a c)")
                    dve.tensor_tensor(yt, bank_o(t)[:, 0:C], yt, ALU.add).then_inc(v_y, 1)
                    if t.after(1):
                        dve.wait_ge(v_mv2, t.n)
                    wait_apart(dve, v_y, t.n + 1)
                    dve.bn_stats(st2[:, :], yt).then_inc(v_st2, 1)
                    if t.after(1):
                        dve.wait_ge(g_ve2, t.n)
                        dve.wait_ge(v_xl, t.n)
                    wait_apart(dve, v_st2, t.n + 1)
                    dve.bn_aggr(mv2[:, :], st2[:, :]).then_inc(v_mv2, 1)
                t = Tile(i, r - 2)
                if t.there():
                    dve.wait_ge(p_pos, t.n + 1)
                    if t.after(1):
                        dve.wait_ge(v_sp, t.n)
                    dve.tensor_tensor(slot_e[:, :], bank7[:, 0:E], region, ALU.add).then_inc(v_pos, 1)
                    dve.tensor_tensor(seen[:, :], seen[:, :], cnt[t.par][:, :], ALU.add).then_inc(v_seen, 1)

            for n in range(NSTEP // 2):
                one_hots(n)
            slot_(-1, 0)
            for n in range(NSTEP // 2, NSTEP):
                one_hots(n)
            slot_(-1, 1)
            dve.wait_ge(s_bload, 16 * NLOAD)
            for raw, parts in ((b1raw, b1parts), (b2raw, b2parts)):
                ins = dve.tensor_copy(parts[0], raw)
            ins.then_inc(s_parts, 1)
            dve.wait_ge(s_parts, 1)
            for raw, parts in ((b1raw, b1parts), (b2raw, b2parts)):
                ins = dve.tensor_tensor(parts[1], raw, parts[0].bitcast(f32), ALU.subtract)
            ins.then_inc(s_parts, 1)
            for s in range(0, 2 * LOOP_A):
                slot_(s // 2, s % 2)
            with dve.Fori(LOOP_A, NCH // 2) as i:
                slot_(i, 0)
                slot_(i, 1)
            for s in range(NCH, LAST + 1):
                slot_(s // 2, s % 2)

            step = [0]

            def then(ins):
                step[0] += 1
                ins.then_inc(v_tab, 1)
                dve.wait_ge(v_tab, step[0])

            dve.wait_ge(s_table, 16)
            dve.wait_ge(p_tot, 1)
            dve.tensor_tensor(pad_f[:, :], bank[0][0:1, 0:E], region[0:1, :], ALU.add)
            then(dve.tensor_scalar(tot_f[:, :], bank[0][0:1, 0:E], float(P - 1), None, ALU.add))
            dve.tensor_copy(pad_i[:, :], pad_f[:, :])
            then(dve.tensor_copy(tot_i[:, :], tot_f[:, :]))
            then(dve.tensor_scalar(nb_i[:, :], tot_i[:, :], 7, None, ALU.arith_shift_right))
            then(dve.tensor_copy(nb_f[:, :], nb_i[:, :]))
            nbb = nb_f[:, :].unsqueeze(1)
            then(dve.tensor_tensor(tri[:, :, :], c_upto,
                                   nbb.to_broadcast([1, E, E]), ALU.mult))
            then(dve.tensor_reduce(last_f[:, :], tri[:, :, :], AX.X, ALU.add))
            then(dve.tensor_tensor(past[:, :, :], c_block,
                                   last_f[:, :].unsqueeze(1).to_broadcast([1, NBLK, E]), ALU.is_ge))
            then(dve.tensor_tensor(past_n[:, :, :], past[:, :, :], nbb.to_broadcast([1, NBLK, E]), ALU.mult))
            dve.tensor_reduce(exp_f[:, :], past[:, :, :], AX.X, ALU.add)
            then(dve.tensor_reduce(base_f[:, :], past_n[:, :, :], AX.X, ALU.add))
            then(dve.scalar_tensor_tensor(out=off_f[:, :], in0=base_f[:, :], scalar=-float(P), in1=c_row,
                                          op0=ALU.mult, op1=ALU.add))
            then(dve.scalar_tensor_tensor(out=base_f[:, :], in0=exp_f[:, :], scalar=float(CAP), in1=off_f[:, :],
                                          op0=ALU.mult, op1=ALU.add))
            dve.tensor_scalar(off_i[:, :], base_f[:, :], float(PADROW), None, ALU.min)
            then(dve.tensor_scalar(exp_i[:, :], exp_f[:, :], float(E - 1), None, ALU.min))
            dve.tensor_tensor(gtmp[:, :], tops[:, :, 1], tops[:, :, 0], ALU.subtract).then_inc(v_gate, 1)
            dve.wait_ge(a_gate, 1)
            then(dve.tensor_scalar(gtmp[:, :], gates[:, 1, :], 1.0, None, ALU.add))
            dve.wait_ge(v_gate, 1)
            dve.reciprocal(gates[:, 0, :], gtmp[:, :]).then_inc(v_gate, 1)
            dve.wait_ge(v_gate, 2)
            dve.tensor_tensor(gates[:, 1, :], gates[:, 1, :], gates[:, 0, :], ALU.mult).then_inc(v_gate, 1)

            dve.memset(xe[REST:REST + 2, :].bitcast(f32), 1.0)

            def x_parts(b, par):
                dve.wait_ge(p_bx, b + 1)
                if not isinstance(b, int) or b >= 1:
                    dve.wait_ge(p_up, b)
                first, rest = bank[0][:, 0:P], bank[0][0:REST, P:2 * P]
                dve.tensor_copy(xh, first)
                dve.tensor_copy(xe[0:REST, :], rest)
                dve.tensor_copy(xm[0:REST, :], rest).then_inc(v_bxh, 1)
                dve.tensor_copy(ring[:, bass.ds(b, 1)], rowin[par][:, C:C + 1].bitcast(i32)).then_inc(v_ring, 1)
                dve.wait_ge(v_bxh, b + 1)
                dve.tensor_tensor(xl, first, xh.bitcast(f32), ALU.subtract)
                dve.tensor_tensor(xm[REST:P, :], rest, xm[0:REST, :].bitcast(f32), ALU.subtract).then_inc(v_bx, 1)

            def lo(b):
                for n in range(2):
                    dve.wait_ge(a_hi, 2 * b + n + 1)
                    dve.tensor_tensor(hTl[:, 3 * n:3 * n + 3, :], up_ps[:, 2 + n, 0:3 * P].rearrange("p (a b) -> p a b", a=3),
                                      hTh[:, 3 * n:3 * n + 3, :].bitcast(f32), ALU.subtract).then_inc(v_lo, 1)

            def y_out(b, par, turn):
                dve.wait_ge(a_ylow, b + 1)
                if not isinstance(b, int) or b >= 2:
                    dve.wait_ge(s_made[par], 16 * turn)
                dve.wait_ge(v_ring, b + 1)
                dve.tensor_copy(dest[par][:, :], ring[:, bass.ds(b, 1)])
                dve.tensor_tensor(yrow[par][:, 0:C], bank[1][:, 0:C], ylow[:, :], ALU.add).then_inc(v_yrow, 1)

            x_parts(0, 0)
            x_parts(1, 1)

            def blk(b, par, turn):
                lo(b)
                if not isinstance(b, int) or b + 2 < NBLK:
                    x_parts(b + 2, par)
                y_out(b, par, turn)

            blk(0, 0, 0)
            blk(1, 1, 0)
            with dve.Fori(1, (NBLK - 2) // 2) as i:
                blk(2 * i, 0, i)
                blk(2 * i + 1, 1, i)
            for b in range((NBLK - 2) // 2 * 2, NBLK):
                blk(b, b % 2, b // 2)

            def gated(t, k):
                if k == 0:
                    if t % 2 == 0:
                        dve.wait_ge(s_back[t // 2], 16)
                    if t >= 4:
                        dve.wait_ge(p_z, t - 3)
                else:
                    dve.wait_ge(v_z1, t + 1)
                dve.scalar_tensor_tensor(out=z[t % 4], in0=back[:, t, k * C:(k + 1) * C], scalar=gates[:, k, t:t + 1],
                                         in1=z[t % 4] if k else ytok[:, t, :], op0=ALU.mult,
                                         op1=ALU.add).then_inc(v_z if k else v_z1, 1)

            dve.wait_ge(v_gate, 3)
            for t in range(0, NT, 2):
                for k in range(2):
                    gated(t, k)
                    gated(t + 1, k)

        @block.tensor
        def _(pe):
            def mm(o, a, b_, start=True, stop=True):
                return pe.matmul(o, a, b_, start=start, stop=stop)

            def gather(n):
                pe.wait_ge(s_hot, n + 1)
                if n >= 2:
                    pe.wait_ge(s_bev, n - 1)
                for k, rows in ((0, P), (1, NREL - P)):
                    for part in (relh, rell):
                        ins = mm(bank[2 + n % 2][0:NH, :], part[0:rows, k, :], hot[n % 2][0:rows, k, :],
                                 start=(k == 0 and part is relh), stop=(k == 1 and part is rell))
                ins.then_inc(s_bmm, 1)

            def position(t, part):
                if not t.there():
                    return
                if t.fixed and t.n == 0:
                    pe.wait_ge(s_bias, 64)
                if t.after(1):
                    pe.wait_ge(v_sub, t.n)
                for j in part:
                    mm(s_ps[:, j, :], ident,
                       bias[:, :, :].rearrange("p (k j h) m -> p k j (h m)", k=2, j=PAIRS)[:, :, j, :])

            def exponentials(t):
                if not t.there():
                    return
                pe.wait_ge(a_exp, t.n + 1)
                if t.last():
                    pe.wait_ge(v_sub, NT)
                if t.after(1) and not t.last():
                    pe.wait_ge(a_pT, t.n)
                if t.after(2) and not t.last():
                    pe.wait_ge(v_pos, t.n - 1)
                if t.there(1):
                    pe.wait_ge(a_v, t.n + 2)
                for j in range(NH // 2):
                    o = banks_pT(t)[j // 3][:, (j % 3) * P:(j % 3 + 1) * P]
                    ins = pe.transpose(o, prob[t.par][:, 2 * j:2 * j + 2, :], ident)
                ins.then_inc(p_pT, 1)

            def slot_(i, r):
                t = Tile(i, r)
                if t.there():
                    pe.wait_ge(a_qk, t.n + 1)
                    for half in range(2):
                        for w in range(2):
                            for j in range(PAIRS):
                                ins = pe.matmul(s_ps[w * L:(w + 1) * L, j, half * P:(half + 1) * P],
                                                qT[32 * j:32 * j + 32, half, w * L:(w + 1) * L],
                                                kbd[32 * j:32 * j + 32, half, w, :, :], start=False, stop=True,
                                                skip_group_check=True)
                    ins.then_inc(p_s, 1)
                t = Tile(i, r + 2)
                if t.there():
                    pe.wait_ge(s_xin, 16 * (t.n + 1))
                    if t.after(1):
                        pe.wait_ge(a_xn, t.n)
                    for k in range(2):
                        ins = pe.transpose(bank[0][:, k * CH:(k + 1) * CH], xin[:, k, :], ident[0:CH, 0:CH])
                    ins.then_inc(p_x, 1)
                if not Tile(i, r - 1).last():
                    exponentials(Tile(i, r - 1))
                t = Tile(i, r + 1)
                if t.there():
                    pe.wait_ge(a_xn, t.n + 1)
                    if t.after(1):
                        pe.wait_ge(a_qk, t.n)
                    for n, w_sb in enumerate((wq, wk)):
                        for half in range(2):
                            for k in range(2):
                                ins = mm(bank[2][0:CH, (2 * n + half) * P:(2 * n + half + 1) * P],
                                         w_sb[:, k, half * CH:(half + 1) * CH], xnT[:, k, :], start=k == 0, stop=k == 1)
                    ins.then_inc(p_qk, 1)
                t = Tile(i, r - 1)
                if t.there():
                    pe.wait_ge(a_pT, t.n + 1)
                    pe.wait_ge(a_v, t.n + 1)
                    if t.after(1) and not t.last():
                        pe.wait_ge(v_y, t.n)
                    for j in range(NH // 2):
                        for w in range(2):
                            ins = mm(bank_o(t)[w * L:(w + 1) * L, j * 2 * (HD + 1):(j + 1) * 2 * (HD + 1)],
                                     pT[:, j, w * L:(w + 1) * L], vbd[t.par][:, w, j, :, :])
                    ins.then_inc(p_o, 1)
                t = Tile(i, r - 2)
                if t.there():
                    pe.wait_ge(v_xl, t.n + 1)
                    if t.there(1):
                        pe.wait_ge(a_pT, t.n + 2)
                    else:
                        pe.wait_ge(v_pos, t.n)
                    for k in range(2):
                        ins = pe.transpose(bank7[0:CH, k * P:(k + 1) * P], row[t.par][0][:, k * CH:(k + 1) * CH], ident)
                    ins.then_inc(p_xl, 1)
                t = Tile(i, r + 1)
                if t.there():
                    if t.after(2):
                        pe.wait_ge(a_pT, t.n - 1)
                    elif t.n == 1:
                        pe.wait_ge(a_v, 1)
                    for k in range(2):
                        ins = mm(bank[3][:, 0:C], xnT[:, k, :], wv[:, k, :], start=k == 0, stop=k == 1)
                    ins.then_inc(p_v, 1)
                position(Tile(i, r + 1), range(1))
                t = Tile(i, r - 1)
                if t.there():
                    pe.wait_ge(v_o, t.n + 1)
                    for k in range(2):
                        ins = pe.transpose(bank_o(t)[0:CH, k * P:(k + 1) * P], osb[:, k * CH:(k + 1) * CH], ident)
                    ins.then_inc(p_oT, 1)
                t = Tile(i, r + 2)
                if t.there():
                    pe.wait_ge(v_xn, t.n + 1)
                    pe.wait_ge(v_x, t.n + 1)
                    for k in range(2):
                        ins = pe.transpose(bank[0][0:CH, k * P:(k + 1) * P], xn[:, k * CH:(k + 1) * CH], ident)
                    ins.then_inc(p_xn, 1)
                t = Tile(i, r - 2)
                if t.there():
                    pe.wait_ge(a_xl, t.n + 1)
                    for k in range(2):
                        ins = mm(bank7[:, 0:E], xlT[0:CH + k, k, :], gw[0:CH + k, k, :], start=k == 0, stop=k == 1)
                    ins.then_inc(p_gate, 1)
                position(Tile(i, r + 1), range(1, PAIRS))
                if Tile(i, r).last():
                    exponentials(Tile(i, r))
                t = Tile(i, r - 1)
                if t.there():
                    pe.wait_ge(a_o, t.n + 1)
                    for k in range(2):
                        ins = mm(bank_o(t)[:, 0:C], oT[0:CH + k, k, :], wo[0:CH + k, k, :], start=k == 0, stop=k == 1)
                    ins.then_inc(p_y, 1)
                t = Tile(i, r - 2)
                if t.there():
                    pe.wait_ge(v_cnt, t.n + 1)
                    if t.after(1):
                        pe.wait_ge(v_seen, t.n)
                    mm(bank7[:, 0:E], earlier[:, :], cnt[t.par][:, :], stop=False)
                    mm(bank7[:, 0:E], ones[:, :], seen[:, :], start=False).then_inc(p_pos, 1)

            pe.wait_ge(s_rel, 2)
            pe.wait_ge(s_set, 2)
            for n in range(NSTEP // 2):
                gather(n)
            slot_(-1, 0)
            for n in range(NSTEP // 2, NSTEP):
                gather(n)
            pe.wait_ge(s_bev, NSTEP)
            pe.wait_ge(s_bload, 16 * NLOAD)
            slot_(-1, 1)
            for s in range(0, 2 * LOOP_A):
                slot_(s // 2, s % 2)
            with pe.Fori(LOOP_A, LOOP_B) as i:
                slot_(i, 0)
                slot_(i, 1)
            for s in range(2 * LOOP_B, LAST):
                slot_(s // 2, s % 2)
            pe.wait_ge(v_seen, NT)
            mm(bank[0][:, 0:E], ones[:, :], seen[:, :]).then_inc(p_tot, 1)

            def expert(b):
                return pe.value_load(exp_i[0:1, bass.ds(b, 1)], min_val=0, max_val=E - 1)

            def rows_in(b, par, done):
                pe.wait_ge(s_rowin[par], done)
                if not isinstance(b, int) or b >= 1:
                    pe.wait_ge(v_bx, b)
                pe.transpose(bank[0][:, 0:P], rowin[par][:, 0:P], ident)
                ins = pe.transpose(bank[0][0:REST, P:2 * P], rowin[par][:, P:C], ident)
                ins.then_inc(p_bx, 1)

            def up(b, e):
                pe.wait_ge(v_bx, b + 1)
                if not isinstance(b, int) or b >= 1:
                    pe.wait_ge(a_gelu, b)
                products = [(xh, w1h, P), (xl, w1h, P), (xh, w1l, P), (xm, w1m, P), (xe, w1e, REST + 2)]
                for n in range(2):
                    for k, (part, w_sb, rows) in enumerate(products):
                        w_e = w_sb[0:rows, :, :].rearrange("p a f -> p (a f)")[:, bass.ds(e * F + n * HW_F, HW_F)]
                        ins = mm(up_ps[:, n, 0:HW_F], part[0:rows, :], w_e, start=k == 0, stop=k == len(products) - 1)
                ins.then_inc(p_up, 1)

            def hidT(b):
                pe.wait_ge(a_gelu, b + 1)
                if not isinstance(b, int) or b >= 1:
                    pe.wait_ge(v_lo, 2 * b)
                for f in range(FT):
                    ins = pe.transpose(up_ps[:, 2 + f // 3, (f % 3) * P:(f % 3 + 1) * P], hid[:, f * P:(f + 1) * P], ident)
                ins.then_inc(p_hT, 1)

            def down(b, e):
                if not isinstance(b, int) or b >= 1:
                    pe.wait_ge(v_yrow, b)
                at2 = e * (FT * 2 * C)
                w2f = w2s[:, :, :].rearrange("p a c -> p (a c)")
                for f in range(FT):
                    if f % 3 == 0:
                        pe.wait_ge(v_lo, 2 * b + f // 3 + 1)
                    mm(bank[1][:, 0:2 * C], hTh[:, f, :], w2f[:, bass.ds(at2 + f * 2 * C, 2 * C)], start=f == 0, stop=False)
                    mm(bank[1][:, 0:C], hTl[:, f, :], w2f[:, bass.ds(at2 + f * 2 * C, C)], start=False, stop=False)
                mm(bank[1][:, 0:C], ones2[:, :], b2r[:, bass.ds(e * C, C)], start=False, stop=True).then_inc(p_dn, 1)

            pe.wait_ge(v_tab, TAB_BLOCKS)
            pe.wait_ge(s_lo, NCH)
            pe.wait_ge(s_rows, 16 * 4)
            e_now = expert(0)
            rows_in(0, 0, 16)
            up(0, e_now)
            rows_in(1, 1, 16)

            def blk(b, par, nxt, done):
                hidT(b)
                if nxt >= 1:
                    up(b + 1, expert(b + 1))
                if nxt >= 2:
                    rows_in(b + 2, par, done)
                down(b, expert(b))

            blk(0, 0, 2, 32)
            blk(1, 1, 2, 32)
            with pe.Fori(1, (NBLK - 2) // 2) as i:
                blk(2 * i, 0, 2, 16 * i + 32)
                blk(2 * i + 1, 1, 2, 16 * i + 32)
            for b in range((NBLK - 2) // 2 * 2, NBLK):
                blk(b, b % 2, min(2, NBLK - 1 - b), 16 * (b // 2) + 32)

            for t in range(NT):
                pe.wait_ge(v_z, t + 1)
                if t % 2 == 0 and t >= 4:
                    pe.wait_ge(a_z, t // 2 - 1)
                for k in range(2):
                    ins = pe.transpose(bank[2 + t // 2 % 2][0:CH, (2 * k + t % 2) * P:(2 * k + t % 2 + 1) * P],
                                       z[t % 4][:, k * CH:(k + 1) * CH], ident)
                ins.then_inc(p_z, 1)



_OUT = ((B, C, IMG, IMG), "float32")


def kernel(x, L0_conv_Wq, L0_conv_Wk, L0_conv_Wv, L0_conv_Wo_w, L0_conv_Wo_b, L0_conv_rel_pos_bias,
           L0_conv_rel_coords, L0_ffn_gate_w, L0_ffn_gate_b, L0_ffn_w1, L0_ffn_b1, L0_ffn_w2, L0_ffn_b2):
    import concourse.bacc as _bacc
    from concourse.bass_utils import run_bass_kernel_spmd as _run

    c, table, places = constants()
    arrays = {
        "x": x, "wqT": np.asarray(L0_conv_Wq).T, "wkT": np.asarray(L0_conv_Wk).T, "wvT": np.asarray(L0_conv_Wv).T,
        "woT": np.asarray(L0_conv_Wo_w).T, "wo_b": L0_conv_Wo_b, "relT": np.asarray(L0_conv_rel_pos_bias).T,
        "coords": np.asarray(L0_conv_rel_coords).reshape(-1), "gate_w": L0_ffn_gate_w, "gate_b": L0_ffn_gate_b,
        "w1": L0_ffn_w1, "b1": L0_ffn_b1, "w2": L0_ffn_w2, "b2": L0_ffn_b2, "const_d": c, "table_d": table, "place_d": places,
    }
    arrays = {f"in_{n}": np.ascontiguousarray(a) for n, a in arrays.items()}
    nc = _bacc.Bacc("TRN2", target_bir_lowering=False, num_devices=1)
    args = [nc.dram_tensor(n, a.shape, mybir.dt.from_np(a.dtype), kind="ExternalInput").ap() for n, a in arrays.items()]
    args.append(nc.dram_tensor("out_0", _OUT[0], mybir.dt.from_np(np.dtype(_OUT[1])), kind="ExternalOutput").ap())
    program(nc, *args)
    r = _run(nc, [arrays], core_ids=[0])
    return r.results[0]["out_0"]
```
